# Optimizing a Trainium2 kernel written in Bass

```python
import numpy as np
import jax
import jax.numpy as jnp

def _softmax(x, axis=-1):
    return jax.nn.softmax(x, axis=axis)

def _gelu(x):
    return jax.nn.gelu(x, approximate=True)

def _silu(x):
    return jax.nn.silu(x)

def _sigmoid(x):
    return jax.nn.sigmoid(x)

def _layernorm(x, axis=-1, eps=1e-05):
    m = jnp.mean(x, axis=axis, keepdims=True)
    v = jnp.var(x, axis=axis, keepdims=True)
    return (x - m) / jnp.sqrt(v + eps)

def _scatter_add(tgt, idx, src, axis=0):
    return tgt.at[idx].add(src)

def _segment_sum(src, seg, n):
    return jax.ops.segment_sum(src, seg, n)
kernel_name = 'mk_adaln_d1_jaxref_r8_a4953c'

def setup_inputs(seed: int=0):
    np.random.seed(seed)
    _w = jnp.asarray

    def _L0_attn_setup():
        import jax, jax.numpy as jnp
        import numpy as np
        import math
        DIM_EMBD = 128
        N_HEADS = 16
        DIM_HEAD = DIM_EMBD // N_HEADS
        LAMBDA_INIT = 0.8
        EPS = 1e-05
        key = jax.random.key(seed)
        ks = jax.random.split(key, 9)
        B, N = (2, 256)
        d2 = 2 * DIM_HEAD * N_HEADS
        xavier = lambda k, shp: jax.random.uniform(k, shp, jnp.float32, -1.0, 1.0) * math.sqrt(6.0 / (shp[0] + shp[1]))
        return {'X': jax.random.normal(ks[0], (B, N, DIM_EMBD), jnp.float32), 'W_q': xavier(ks[1], (d2, DIM_EMBD)), 'W_k': xavier(ks[2], (d2, DIM_EMBD)), 'W_v': xavier(ks[3], (d2, DIM_EMBD)), 'W_o': xavier(ks[4], (DIM_EMBD, d2)), 'lambda_q1': jax.random.normal(ks[5], (N_HEADS, DIM_HEAD), jnp.float32), 'lambda_k1': jax.random.normal(ks[6], (N_HEADS, DIM_HEAD), jnp.float32), 'lambda_q2': jax.random.normal(ks[7], (N_HEADS, DIM_HEAD), jnp.float32), 'lambda_k2': jax.random.normal(ks[8], (N_HEADS, DIM_HEAD), jnp.float32), 'rms_scale': jnp.ones((2 * DIM_HEAD,), jnp.float32)}
    _L0_attn_in = _L0_attn_setup()

    def _L0_ffn_setup():
        import jax, jax.numpy as jnp
        import numpy as np
        TOP_K = 2
        NUM_EXPERTS = 8
        B, T, H, F = (4, 256, 128, 512)
        key = jax.random.key(seed)
        ks = jax.random.split(key, 6)
        s_in = 1.0 / np.sqrt(H)
        s_ff = 1.0 / np.sqrt(F)
        return {'x': jax.random.normal(ks[0], (B, T, H), dtype=jnp.float32), 'router_w': jax.random.normal(ks[1], (NUM_EXPERTS, H), dtype=jnp.float32) * s_in, 'router_b': jax.random.normal(ks[2], (NUM_EXPERTS,), dtype=jnp.float32) * 0.01, 'gate_w': jax.random.normal(ks[3], (NUM_EXPERTS, F, H), dtype=jnp.float32) * s_in, 'up_w': jax.random.normal(ks[4], (NUM_EXPERTS, F, H), dtype=jnp.float32) * s_in, 'down_w': jax.random.normal(ks[5], (NUM_EXPERTS, H, F), dtype=jnp.float32) * s_ff}
    _L0_ffn_in = _L0_ffn_setup()
    _L0_c = _w((lambda *s: np.random.randn(*s).astype(np.float32) * 0.05)(32, 128))
    _L0_wmod = _w((lambda *s: np.random.randn(*s).astype(np.float32) * 0.05)(128, 6 * 128) * 128 ** (-0.5))
    _d = {'L0_attn_X': _L0_attn_in['X'], 'L0_attn_W_q': _L0_attn_in['W_q'], 'L0_attn_W_k': _L0_attn_in['W_k'], 'L0_attn_W_v': _L0_attn_in['W_v'], 'L0_attn_W_o': _L0_attn_in['W_o'], 'L0_attn_lambda_q1': _L0_attn_in['lambda_q1'], 'L0_attn_lambda_k1': _L0_attn_in['lambda_k1'], 'L0_attn_lambda_q2': _L0_attn_in['lambda_q2'], 'L0_attn_lambda_k2': _L0_attn_in['lambda_k2'], 'L0_attn_rms_scale': _L0_attn_in['rms_scale'], 'L0_ffn_router_w': _L0_ffn_in['router_w'], 'L0_ffn_router_b': _L0_ffn_in['router_b'], 'L0_ffn_gate_w': _L0_ffn_in['gate_w'], 'L0_ffn_up_w': _L0_ffn_in['up_w'], 'L0_ffn_down_w': _L0_ffn_in['down_w'], 'L0_c': _L0_c, 'L0_wmod': _L0_wmod}
    _x0 = _d['L0_attn_X']
    _d['L0_attn_X'] = jax.random.normal(jax.random.fold_in(jax.random.key(seed), 1), (32, 256, 128), dtype=_x0.dtype)
    del _x0
    return _d

def reference(L0_attn_X, L0_attn_W_q, L0_attn_W_k, L0_attn_W_v, L0_attn_W_o, L0_attn_lambda_q1, L0_attn_lambda_k1, L0_attn_lambda_q2, L0_attn_lambda_k2, L0_attn_rms_scale, L0_ffn_router_w, L0_ffn_router_b, L0_ffn_gate_w, L0_ffn_up_w, L0_ffn_down_w, L0_c, L0_wmod):

    def _L0_attn_ref(X, W_q, W_k, W_v, W_o, lambda_q1, lambda_k1, lambda_q2, lambda_k2, rms_scale):
        import jax, jax.numpy as jnp
        import numpy as np
        import math
        DIM_EMBD = 128
        N_HEADS = 16
        DIM_HEAD = DIM_EMBD // N_HEADS
        LAMBDA_INIT = 0.8
        EPS = 1e-05
        B, N, _ = X.shape
        H, dh = (N_HEADS, DIM_HEAD)

        def split_heads(Y):
            return Y.reshape(B, N, H, 2 * dh).transpose(0, 2, 1, 3)
        Q = split_heads(X @ W_q.T)
        K = split_heads(X @ W_k.T)
        V = split_heads(X @ W_v.T)
        Q1, Q2 = (Q[..., :dh], Q[..., dh:])
        K1, K2 = (K[..., :dh], K[..., dh:])
        lam = jnp.exp(jnp.sum(lambda_q1 * lambda_k1, -1)) - jnp.exp(jnp.sum(lambda_q2 * lambda_k2, -1)) + LAMBDA_INIT
        lam = lam[None, :, None, None]
        scaling = 1.0 / math.sqrt(dh)
        causal = jnp.tril(jnp.ones((N, N), jnp.bool_))
        neg_inf = jnp.float32(-jnp.inf)
        A1 = jnp.einsum('bhqd,bhkd->bhqk', Q1, K1) * scaling
        A2 = jnp.einsum('bhqd,bhkd->bhqk', Q2, K2) * scaling
        A1 = jnp.where(causal, A1, neg_inf)
        A2 = jnp.where(causal, A2, neg_inf)
        attn = jax.nn.softmax(A1, -1) - lam * jax.nn.softmax(A2, -1)
        O = jnp.einsum('bhqk,bhkd->bhqd', attn, V)
        rms = jnp.sqrt(jnp.mean(O * O, -1, keepdims=True) + EPS)
        O = O / rms * rms_scale * (1.0 - LAMBDA_INIT)
        O = O.transpose(0, 2, 1, 3).reshape(B, N, H * 2 * dh)
        return O @ W_o.T

    def _L0_ffn_ref(x, router_w, router_b, gate_w, up_w, down_w):
        import jax, jax.numpy as jnp
        import numpy as np
        TOP_K = 2
        NUM_EXPERTS = 8
        B, T, H, F = (4, 256, 128, 512)
        logits = jnp.einsum('bth,eh->bte', x, router_w) + router_b
        topv, topi = jax.lax.top_k(logits, TOP_K)
        gates = jax.nn.softmax(topv, axis=-1)

        def body(acc, inputs):
            e, gw, uw, dw = inputs
            w = jnp.sum(gates * (topi == e), axis=-1)
            h = jax.nn.silu(jnp.einsum('bth,fh->btf', x, gw)) * jnp.einsum('bth,fh->btf', x, uw)
            y = jnp.einsum('btf,hf->bth', h, dw)
            return (acc + y * w[..., None], None)
        init = jnp.zeros_like(x)
        xs = (jnp.arange(NUM_EXPERTS), gate_w, up_w, down_w)
        out, _ = jax.lax.scan(body, init, xs)
        return out
    x = L0_attn_X
    mod = (_silu(L0_c) @ L0_wmod).reshape(L0_c.shape[0], 6, 1, -1)
    sa, ca, ga, sb, cb, gb = (mod[:, 0], mod[:, 1], mod[:, 2], mod[:, 3], mod[:, 4], mod[:, 5])
    ga = (2 * (ga >= 0) - 1) * jnp.maximum(jnp.abs(ga), 0.25)
    gb = (2 * (gb >= 0) - 1) * jnp.maximum(jnp.abs(gb), 0.25)
    h = _layernorm(x, axis=-1) * (1 + ca) + sa
    x = x + ga * _L0_attn_ref(h, L0_attn_W_q, L0_attn_W_k, L0_attn_W_v, L0_attn_W_o, L0_attn_lambda_q1, L0_attn_lambda_k1, L0_attn_lambda_q2, L0_attn_lambda_k2, L0_attn_rms_scale)
    h = _layernorm(x, axis=-1) * (1 + cb) + sb
    x = x + gb * _L0_ffn_ref(h, L0_ffn_router_w, L0_ffn_router_b, L0_ffn_gate_w, L0_ffn_up_w, L0_ffn_down_w)
    return x

_drawn_inputs = setup_inputs


def setup_inputs(seed=0):
    import zlib

    import numpy as np

    out = dict(_drawn_inputs(seed))
    spreads = {'L0_attn_rms_scale': (1.0, 0.6)}
    factors = {'L0_ffn_router_b': 22.641}
    for name, (base, spread) in spreads.items():
        noise = np.random.default_rng([zlib.crc32(name.encode()), seed]).standard_normal(out[name].shape)
        drawn = base * np.exp(spread * noise) if base else spread * noise
        out[name] = jnp.asarray(drawn.astype(out[name].dtype))
    for name, factor in factors.items():
        out[name] = (out[name] * factor).astype(out[name].dtype)
    return out
```

```python
import concourse.bass as bass
from concourse import mybir
from contextlib import ExitStack
import numpy as np

F32 = mybir.dt.float32
BF16 = mybir.dt.bfloat16
I32 = mybir.dt.int32
U32 = mybir.dt.uint32
ALU = mybir.AluOpType
ACT = mybir.ActivationFunctionType
AX = mybir.AxisListType

P = 128
NB, SEQ, DIM = 32, 256, 128
NH, DH = 16, 8
NT = SEQ // P
NE, FF = 8, 512
FCH = FF // P
TILES = NB * NT
HU = NH // 2
EPS = 1e-5
LAMBDA_INIT = 0.8
SCALE = DH ** -0.5
NEG = -1e30
SLOTS = 6
HALF_ROWS = SLOTS * DH
QK_ROWS = 2 * HALF_ROWS
MAX_ROWS = 2 * 3
ALL_ROWS = QK_ROWS + MAX_ROWS
Q_SLOTS = (0, 0, 0, 1, 1, 2)
K_RUNS = ((0, 3), (3, 2), (5, 1))
VW = 32
ROUTED = 2 * NB * SEQ
REGION = NB * SEQ + P
RING = 8
FFN_TILES = -(-(ROUTED // P + NE - 1) // RING) * RING
LAST_PADS = FFN_TILES - ROUTED // P + 1
SORTED_ROWS = NE * REGION + LAST_PADS * P
RW = DIM + 2
SKIPPED = 1 << 20

BANK = 512
PAIRS = NH // 2
NBANKS = 3 * PAIRS
SETUP_LAM, SETUP_SILU, SETUP_ROWS, SETUP_DONE = 6, 9, 19, 21
ROUTE_DIFF, ROUTE_BOTH, ROUTE_CARRY, ROUTE_ROWS, ROUTE_STEPS = 6, 9, 12, 16, 17
NEWTON = 12


class Batch:

    def __init__(self, pair, c):
        self.pair_reg, self.c = pair, c
        self.static = pair is None
        self.n = c if pair is None else pair * 2 + c
        self.par = c % 2
        self.half = c // 2 if pair is None else pair + c // 2

    def plus(self, d):
        return Batch(self.pair_reg, self.c + d)


class Event:

    def __init__(self, sem, per=1):
        self.sem, self.per = sem, per

    def at(self, b, k=None):
        return b.n * self.per + (self.per if k is None else k)


def wait(eng, event, b, k=None):
    if b.static and (b.c < 0 or event.at(b, k) <= 0):
        return
    assert b.c * event.per + (event.per if k is None else k) > 0
    eng.wait_ge(event.sem, event.at(b, k))


def wait_half(eng, event, b):
    if b.static and b.c < 0:
        return
    assert b.c >= 0
    eng.wait_ge(event.sem, (b.half + 1) * event.per)


def adaln_block(nc, x, w_qk, w_v, w_o, lambdas, rms_col, router_w, router_b, gate_w, up_w, down_w,
                c_t, w_mod, ident, mask_q, before, iota, ramp, pair_no, tile_no, filler, out):
    ctx = ExitStack()
    with ctx:
        def sb(name, shape, dt=F32):
            return ctx.enter_context(nc.sbuf_tensor(name, shape, dt))

        def ps(name, shape, dt=F32):
            return ctx.enter_context(nc.psum_tensor(name, shape, dt))

        def sem(name):
            return ctx.enter_context(nc.semaphore(name))

        def ev(name, per=1):
            return Event(sem(name), per)

        def dram(name, shape, dt=F32):
            return nc.dram_tensor(name, shape, dt, kind="Internal").ap()

        q_parts = dram("q_parts", [NB, 2, SLOTS, DH, NH, SEQ], BF16)
        k_parts = dram("k_parts", [NB, 2, 3, DH, NH, SEQ], BF16)
        max_parts = dram("max_parts", [NB, 2, MAX_ROWS, HU, SEQ], BF16)
        mod_rows = dram("mod_rows", [NB, 4 * DIM])
        rows_sorted = dram("rows_sorted", [SORTED_ROWS, RW])
        pair_out = dram("pair_out", [ROUTED, DIM])

        idf = sb("idf", [P, P])
        idb = sb("idb", [P, P], BF16)
        mask4 = sb("mask4", [P, 4, P], BF16)
        beforeb = sb("beforeb", [P, P], BF16)
        onesb = sb("onesb", [P, P], BF16)
        iota8 = sb("iota8", [P, NE])
        wqk = sb("wqk", [P, 4, P])
        wv = sb("wv", [P, NH * 2 * DH])
        wo = sb("wo", [P, 2, DIM])
        rmsc = sb("rmsc", [P, 1])
        rw = sb("rw", [P, NE])
        rb = sb("rb", [P, NE])
        lams = sb("lams", [P, 2, NH])
        neg_lam = sb("neg_lam", [P, NH])
        ct = sb("ct", [P, NB])
        silu_t = sb("silu_t", [P, 3, NB])
        sa_t = sb("sa_t", [P, NB])
        ca_t = sb("ca_t", [P, NB])
        mrow = sb("mrow", [NB, 4, DIM])
        wg = sb("wg", [P, NE * FF])
        wu = sb("wu", [P, NE * FF])
        wd = sb("wd", [P, NE * FF])

        xres = sb("xres", [P, TILES * DIM])

        qt = sb("qt", [P, 4, HU, SEQ], BF16)
        kt = sb("kt", [P, 4, 2, HU, SEQ], BF16)
        probs = sb("probs", [P, 2, 3, BANK])
        v = sb("v", [P, 2, NT, NH, VW])
        xn = sb("xn", [P, NT, DIM])
        ht = sb("ht", [P, 2, SEQ])
        part_h = sb("part_h", [P, 2, 2 * SEQ], BF16)
        part_m = sb("part_m", [P, 2, 2 * SEQ], BF16)
        part_l = sb("part_l", [P, 2, 2 * SEQ], BF16)
        rest = sb("rest", [P, 2, 2 * SEQ])
        mx = sb("mx", [P, 2, NT, 2, HU])
        mrest = sb("mrest", [P, NT * 2, HU])
        nm = sb("nm", [P, 2, NT * 2, 3, HU], BF16)
        nmt = sb("nmt", [MAX_ROWS * HU, 2, SEQ], BF16)
        ot = sb("ot", [P, 2, 4, SEQ])
        rec = sb("rec", [P, 2 * HU])
        on2 = sb("on2", [P, NT, NH, 2, 2 * DH])
        o = sb("o", [P, NT * NH, 2 * DH])
        on_tok = sb("on_tok", [P, NT, NH * 2 * DH])
        rms_ss = sb("rms_ss", [P, NT * NH])
        osq = sb("osq", [P, NT * NH, 2 * DH])
        ont = sb("ont", [P, 2, SEQ])
        stats = sb("stats", [P, 2, NT, 6])
        mv1 = sb("mv1", [P, NT, 2])
        mv2 = sb("mv2", [P, NT, 2])
        NV = NT * NH + 2 * NT
        var = sb("var", [P, NV])
        rstd = sb("rstd", [P, NV])
        nt1 = sb("nt1", [P, NV])
        nt2 = sb("nt2", [P, NV])
        mods = sb("mods", [P, 2, 3, DIM])
        xtmp = sb("xtmp", [P, NT, DIM])
        h2 = sb("h2", [P, 2, 2, NT, RW])
        h2t = sb("h2t", [P, SEQ])
        lg = sb("lg", [P, NT, NE])
        top8 = sb("top8", [P, NT, 8])
        top8i = sb("top8i", [P, NT, 8], U32)
        topf = sb("topf", [P, 2, NT])
        chosen = sb("chosen", [P, 2 * NT, NE])
        both = sb("both", [P, NT, NE], BF16)
        gdiff = sb("gdiff", [P, NT])
        gexp = sb("gexp", [P, NT])
        gden = sb("gden", [P, NT])
        carry = sb("carry", [P, NE])
        pos = sb("pos", [P, NT, NE])
        posm = sb("posm", [P, 2 * NT, NE])
        posf = sb("posf", [P, 2 * NT])
        idx = sb("idx", [P, 2, 2 * NT], I32)
        pairno = sb("pairno", [P, 2 * NT])
        posm_ramp = sb("posm_ramp", [P, NE])
        ends = sb("ends", [P, NE])
        endi = sb("endi", [P, NE], I32)
        ntil = sb("ntil", [P, NE])
        first = sb("first", [P, NE])
        jump = sb("jump", [P, NE])
        tileno = sb("tileno", [P, FFN_TILES])
        fill = sb("fill", [P, RW])
        tile_row = sb("tile_row", [P, FFN_TILES], I32)
        tile_exp = sb("tile_exp", [P, FFN_TILES], I32)

        maskf = ont[:, 0, 0:P]
        beforef = ont[:, 1, 0:P]
        lamv = rest[:, 0, :].rearrange("p (j k) -> p j k", j=4)
        mtmp = rest[0:NB, 1, 0:2 * DIM].rearrange("p (j k) -> p j k", j=2)
        w_mod_sb = probs[:, 0, 0:2, :].rearrange("p a k -> p (a k)")[:, 0:6 * DIM]

        p_exp = ps("p_exp", [P, 3, BANK])
        p_max = ps("p_max", [P, 2, 2 * SEQ])
        p_out = ps("p_out", [P, 2, SEQ])
        p_mix = ps("p_mix", [P, 2, 2 * SEQ])

        consts_loaded = sem("consts_loaded")
        waits_met = sem("waits_met")
        ffn_w_loaded = sem("ffn_w_loaded")
        setup_v = sem("setup_v")
        setup_a = sem("setup_a")
        setup_t = sem("setup_t")
        mods_saved = sem("mods_saved")
        x_loaded = [ev(f"x_loaded{i}", 16) for i in range(2)]
        mods_loaded = [ev(f"mods_loaded{i}", 16) for i in range(2)]
        stats1 = ev("stats1", NT + NT)
        xn_ready = ev("xn_ready", NT)
        xt_ps = ev("xt_ps")
        ht_ready = ev("ht_ready")
        proj_ps = ev("proj_ps", 2)
        h_ready = ev("h_ready", 2)
        r_ready = ev("r_ready", 2)
        m_ready = ev("m_ready", 2)
        l_ready = ev("l_ready", 2)
        NSAVE = SLOTS + 3
        parts_saved = ev("parts_saved", 16 * NSAVE)
        NLOAD = 1 + 2 * len(K_RUNS)
        unit_loaded = [ev(f"unit_loaded{w}", 16 * NLOAD) for w in range(2)]
        v_ps = ev("v_ps")
        v_ready = ev("v_ready")
        max_ps = ev("max_ps", NBANKS)
        max_done = ev("max_done", NBANKS)
        nm_step = ev("nm_step", 2 * 4)
        nm_ps = ev("nm_ps", 2)
        nmt_ready = ev("nmt_ready", 2)
        nm_saved = ev("nm_saved", 32)
        nm_loaded = [ev(f"nm_loaded{w}", 16) for w in range(2)]
        exp_ps = ev("exp_ps", NBANKS)
        exp_done = ev("exp_done", NBANKS)
        masked = ev("masked", NBANKS)
        pv_done = ev("pv_done", PAIRS)
        ot_ready = ev("ot_ready", PAIRS // 2)
        ot_ps = ev("ot_ps", 4)
        rec_step = ev("rec_step", 8)
        on2_ready = ev("on2_ready", 4)
        o_ready = ev("o_ready")
        osq_ready = ev("osq_ready")
        rms_sum = ev("rms_sum")
        newton = sem("newton")
        on_ready = ev("on_ready")
        ont_ps = ev("ont_ps")
        ont_ready = ev("ont_ready")
        wo_ps = ev("wo_ps")
        attn_scaled = ev("attn_scaled")
        x1_ready = ev("x1_ready")
        stats2 = ev("stats2", NT + NT)
        xn2_ready = ev("xn2_ready", NT)
        h2_step = ev("h2_step", 2)
        h2_copied = ev("h2_copied")
        h2t_ps = ev("h2t_ps")
        h2t_ready = ev("h2t_ready")
        lg_ps = ev("lg_ps")
        route = ev("route", ROUTE_STEPS)
        gexp_ready = ev("gexp_ready")
        rank_ps = ev("rank_ps")
        scattered = [ev(f"scattered{i}", 64) for i in range(2)]

        tables = sem("tables")
        filled = sem("filled")
        rows_loaded = [sem(f"rows_loaded{r}") for r in range(RING)]
        row_t_ps = sem("row_t_ps")
        row_t_ready = sem("row_t_ready")
        gate_ps = sem("gate_ps")
        up_ps = sem("up_ps")
        gate_done = sem("gate_done")
        hid_ready = sem("hid_ready")
        hid_t_ps = sem("hid_t_ps")
        hid_t_ready = sem("hid_t_ready")
        down_ps = sem("down_ps")
        rows_ready = sem("rows_ready")
        pairs_stored = [sem(f"pairs_stored{r}") for r in range(RING)]
        fin_loaded = [ev(f"fin_loaded{i}", 48) for i in range(2)]
        fin_step = ev("fin_step", 3)
        fin_stored = [ev(f"fin_stored{i}", 16) for i in range(2)]

        block = ctx.enter_context(nc.Block())

        CONSTS = 20
        LEAD, TAIL = 4, 3
        FIRST_FULL, LAST_FULL = TAIL + 1, NB - 1 - LEAD
        LOOPED = (LAST_FULL - FIRST_FULL + 1) // 2 * 2

        def iterations(eng, body):
            for i in range(-LEAD, FIRST_FULL):
                body(Batch(None, i))
            base = FIRST_FULL
            with eng.Fori(0, LOOPED // 2) as pair:
                body(Batch(pair, base))
                body(Batch(pair, base + 1))
            for i in range(base + LOOPED, NB + TAIL):
                body(Batch(None, i))

        def settle(eng):
            eng.sem_inc(waits_met, 1)

        def active(b):
            return not b.static or 0 <= b.c < NB

        MISC0 = [(ht_ready, 1, 2), (r_ready, 1, 2), (r_ready, 2, 2), (on2_ready, 4, -1),
                 (v_ready, 1, 1), (on2_ready, 1, 0)]
        MISC1 = [(ont_ready, 1, -2), (attn_scaled, 1, -2), (nmt_ready, 2, 0), (on2_ready, 3, -1),
                 (h2t_ready, 1, -3), (route, 1, -3), (nmt_ready, 1, 1), (route, ROUTE_CARRY, -3),
                 (on2_ready, 2, 0)]

        def mix_free(pe, i, bank, turn):
            readers = (MISC0, MISC1)[bank]
            for back in range(1, 4 * len(readers)):
                event, k, d = readers[(turn - back) % len(readers)]
                b = i.plus(d + (turn - back) // len(readers))
                if active(b):
                    wait(pe, event, b, k)
                    return
                if b.static and b.c < 0 and back > 3 * len(readers):
                    return


        pool_f = kt[:].rearrange("p a t h k -> p (a t h k)").bitcast(F32)

        def carve(start, *shape):
            n = int(np.prod(shape))
            names = "abc"[:len(shape)]
            view = pool_f[:, start:start + n]
            if len(shape) > 1:
                view = view.rearrange("p (" + " ".join(names) + ") -> p " + " ".join(names),
                                      **dict(zip(names, shape)))
            return view, start + n

        rows_in, at = carve(0, RING, RW)
        rows_t, at = carve(at, 2, P)
        act_g, at = carve(at, 2, FF)
        hid, at = carve(at, 2, FF)
        hid_t, at = carve(at, 2, FF)
        rows_out, at = carve(at, RING, DIM)
        assert at <= 4 * 2 * HU * SEQ // 2
        p_gate = p_exp[:, 0:2, :]
        p_up = p_max
        p_hid_t = p_mix
        p_row_t = p_out[:, 0, 0:P]
        p_down = p_exp[:, 2, 0:DIM]
        pair_view = probs[:].rearrange("p a b k -> p (a b k)")
        NF = 2 * NT * DIM
        fin_in = pair_view[:, 0:2 * NF].rearrange("p (a j c) -> p a j c", a=2, j=2)
        fin_gb = pair_view[:, 2 * NF:2 * NF + 2 * DIM].rearrange("p (a c) -> p a c", a=2)
        fin_out = pair_view[:, 2 * NF + 2 * DIM:2 * NF + 2 * DIM + 2 * NT * DIM].rearrange("p (a c) -> p a c", a=2)

        class Tile:

            def __init__(self, reg, c):
                self.static = reg is None
                self.reg, self.c = reg, c
                self.n = c if reg is None else reg * RING + c
                self.slot = c % RING
                self.turn = c // RING if reg is None else reg + c // RING

            def plus(self, d):
                return Tile(self.reg, self.c + d)

        def t_active(j):
            return not j.static or 0 <= j.c < FFN_TILES

        def t_wait(eng, s, j, per=1, k=None):
            v = j.n * per + (per if k is None else k)
            if j.static and (j.c < 0 or v <= 0):
                return
            eng.wait_ge(s, v)

        def tiles(eng, body):
            for c in range(-1, RING):
                body(Tile(None, c))
            with eng.Fori(1, FFN_TILES // RING - 1) as reg:
                for c in range(RING):
                    body(Tile(reg, c))
            for c in range(FFN_TILES - RING, FFN_TILES + 2):
                body(Tile(None, c))

        TABLE_STEPS = 17

        def ffn_sp(sp):
            sp.wait_ge(tables, 1)
            for e in range(NE):
                start = sp.value_load(endi[0:1, e:e + 1], min_val=0, max_val=SORTED_ROWS - LAST_PADS * P)
                if e < NE - 1:
                    sp.dma_start(rows_sorted[bass.ds(start, P), :], fill[:, :]).then_inc(filled, 16)
                else:
                    sp.dma_start(rows_sorted[bass.ds(start, LAST_PADS * P), :].rearrange("(m p) r -> p m r", p=P),
                                 fill[:].unsqueeze(1).to_broadcast([P, LAST_PADS, RW])).then_inc(filled, 16)
            sp.wait_ge(tables, TABLE_STEPS)
            sp.wait_ge(filled, 16 * NE)
            for i in range(2):
                sp.wait_ge(scattered[i].sem, scattered[i].per * NB // 2)
            sp.wait_ge(pv_done.sem, PAIRS * NB)

            def load(j):
                if not t_active(j):
                    return
                if not (j.static and j.c < RING):
                    sp.wait_ge(pairs_stored[j.slot], 16 * j.turn)
                row = sp.value_load(tile_row[0:1, bass.ds(j.n, 1)], min_val=0, max_val=SORTED_ROWS - P)
                sp.dma_start(rows_in[:, j.slot, :], rows_sorted[bass.ds(row, P), :]).then_inc(rows_loaded[j.slot], 16)

            for c in range(RING):
                load(Tile(None, c))
            with sp.Fori(1, FFN_TILES // RING) as reg:
                for c in range(RING):
                    load(Tile(reg, c))
            for r in range(RING):
                sp.wait_ge(pairs_stored[r], 16 * (FFN_TILES // RING))

            def final(b):
                wait(sp, fin_step, b.plus(-2))
                for j in range(2):
                    sp.dma_start(fin_in[:, b.par, j, :].rearrange("p (t c) -> p t c", t=NT),
                                 pair_out[bass.ds(b.n * SEQ + j * NB * SEQ, SEQ), :].rearrange("(t p) c -> p t c", p=P)
                                 ).then_inc(fin_loaded[b.par].sem, 16)
                sp.dma_start(fin_gb[:, b.par, :], mod_rows[bass.ds(b.n, 1), 3 * DIM:4 * DIM].to_broadcast([P, DIM])
                             ).then_inc(fin_loaded[b.par].sem, 16)

            for c in range(2):
                final(Batch(None, c))
            with sp.Fori(0, NB // 2 - 1) as pair:
                for c in range(2):
                    final(Batch(pair, c + 2))

        def ffn_products(pe):
            pe.wait_ge(ffn_w_loaded, 48)
            pe.wait_ge(tables, TABLE_STEPS)

            def body(j):
                j1, jt, jd = j.plus(1), j.plus(-1), j.plus(-2)
                if t_active(j1):
                    pe.wait_ge(rows_loaded[j1.slot], 16 * (j1.turn + 1))
                    t_wait(pe, row_t_ready, j1.plus(-1))
                    nc.tensor.transpose(p_row_t, rows_in[:, j1.slot, 0:DIM], idf[:]).then_inc(row_t_ps, 1)
                if t_active(j):
                    w0 = pe.value_load(tile_exp[0:1, bass.ds(j.n, 1)], min_val=0, max_val=(NE - 1) * FF)
                    t_wait(pe, row_t_ready, j)
                    t_wait(pe, gate_done, j.plus(-2))
                    nc.tensor.matmul(p_gate[:, j.c % 2, :], rows_t[:, j.c % 2, :], wg[:, bass.ds(w0, FF)],
                                     start=True, stop=True).then_inc(gate_ps, 1)
                    t_wait(pe, hid_ready, j.plus(-2))
                    nc.tensor.matmul(p_up[:, j.c % 2, :], rows_t[:, j.c % 2, :], wu[:, bass.ds(w0, FF)],
                                     start=True, stop=True).then_inc(up_ps, 1)
                if t_active(jt):
                    t_wait(pe, hid_ready, jt)
                    t_wait(pe, hid_t_ready, jt.plus(-2))
                    for f in range(FCH):
                        m = nc.tensor.transpose(p_hid_t[:, jt.c % 2, f * P:(f + 1) * P], hid[:, jt.c % 2, f * P:(f + 1) * P], idf[:])
                    m.then_inc(hid_t_ps, 1)
                if t_active(jd):
                    w0 = pe.value_load(tile_exp[0:1, bass.ds(jd.n, 1)], min_val=0, max_val=(NE - 1) * FF)
                    t_wait(pe, hid_t_ready, jd)
                    t_wait(pe, rows_ready, jd.plus(-1))
                    for f in range(FCH):
                        m = nc.tensor.matmul(p_down, hid_t[:, jd.c % 2, f * P:(f + 1) * P],
                                             wd[:, bass.ds(w0 + f * P, P)], start=(f == 0), stop=(f == FCH - 1))
                    m.then_inc(down_ps, 1)

            tiles(pe, body)

        def ffn_activations(act):
            def body(j):
                jd = j.plus(-2)
                if t_active(j):
                    t_wait(act, gate_ps, j)
                    t_wait(act, hid_ready, j.plus(-2))
                    nc.scalar.activation(act_g[:, j.c % 2, :], p_gate[:, j.c % 2, :], ACT.Silu).then_inc(gate_done, 1)
                if t_active(jd):
                    t_wait(act, down_ps, jd)
                    if not (jd.static and jd.c < RING):
                        act.wait_ge(pairs_stored[jd.slot], 16 * jd.turn)
                    nc.scalar.activation(rows_out[:, jd.slot, :], p_down, ACT.Copy,
                                         scale=rows_in[:, jd.slot, DIM + 1:DIM + 2]).then_inc(rows_ready, 1)

            tiles(act, body)

            def final(b):
                wait(act, fin_step, b)
                act.dma_start(out[bass.ds(b.n, 1)].rearrange("a (t p) c -> p (a t) c", p=P),
                              fin_out[:, b.par, :].rearrange("p (t c) -> p t c", t=NT)).then_inc(fin_stored[b.par].sem, 16)

            for c in range(2):
                final(Batch(None, c))
            with act.Fori(0, NB // 2 - 1) as pair:
                for c in range(2):
                    final(Batch(pair, c + 2))
            for i in range(2):
                act.wait_ge(fin_stored[i].sem, 16 * NB // 2)

        def ffn_vector(dve):
            V = nc.vector
            count = [0]

            def step(ins):
                count[0] += 1
                ins.then_inc(tables, 1)
                dve.wait_ge(tables, count[0])

            dve.wait_ge(route.sem, ROUTE_STEPS * NB)
            step(V.tensor_copy(endi[:], carry[:]))
            step(V.tensor_tensor(ends[:], carry[:], posm_ramp[:], ALU.subtract))
            step(V.tensor_scalar(ntil[:].bitcast(I32), ends[:], float(P - 1), None, ALU.add))
            step(V.tensor_scalar(ntil[:].bitcast(I32), ntil[:].bitcast(I32), P.bit_length() - 1, None, ALU.logical_shift_right))
            step(V.tensor_copy(first[:], ntil[:].bitcast(I32)))
            step(V.tensor_scalar(jump[:], first[:], -float(P), float(REGION), ALU.mult, ALU.add))
            for e in range(1, NE - 1):
                step(V.tensor_tensor(first[:, e:e + 1], first[:, e:e + 1], first[:, e - 1:e], ALU.add))
            ge = pool_f[:, 0:FFN_TILES * (NE - 1)].rearrange("p (j e) -> p j e", e=NE - 1)
            sums = pool_f[:, FFN_TILES * NE:FFN_TILES * (NE + 1)]
            dve.wait_ge(pv_done.sem, PAIRS * NB)
            step(V.tensor_tensor(ge, tileno[:].unsqueeze(2).to_broadcast([P, FFN_TILES, NE - 1]),
                                 first[:, 0:NE - 1].unsqueeze(1).to_broadcast([P, FFN_TILES, NE - 1]), ALU.is_ge))
            step(V.reduce_sum(sums, ge, AX.X))
            V.tensor_scalar(tile_exp[:], sums, float(FF), None, ALU.mult)
            step(V.tensor_tensor(ge, ge, jump[:, 0:NE - 1].unsqueeze(1).to_broadcast([P, FFN_TILES, NE - 1]), ALU.mult))
            step(V.reduce_sum(sums, ge, AX.X))
            step(V.scalar_tensor_tensor(tile_row[:], tileno[:], float(P), sums, ALU.mult, ALU.add))
            assert count[0] == TABLE_STEPS, count

            def body(j):
                j1, jt = j.plus(1), j.plus(-1)
                if t_active(j1):
                    t_wait(dve, row_t_ps, j1)
                    t_wait(dve, up_ps, j1.plus(-2))
                    V.tensor_copy(rows_t[:, j1.c % 2, :], p_row_t).then_inc(row_t_ready, 1)
                if t_active(j):
                    t_wait(dve, gate_done, j)
                    t_wait(dve, up_ps, j)
                    t_wait(dve, hid_t_ps, j.plus(-2))
                    V.tensor_tensor(hid[:, j.c % 2, :], act_g[:, j.c % 2, :], p_up[:, j.c % 2, :], ALU.mult).then_inc(hid_ready, 1)
                if t_active(jt):
                    t_wait(dve, hid_t_ps, jt)
                    t_wait(dve, down_ps, jt.plus(-2))
                    V.tensor_copy(hid_t[:, jt.c % 2, :], p_hid_t[:, jt.c % 2, :]).then_inc(hid_t_ready, 1)

            tiles(dve, body)

            def final(b):
                wait_half(dve, fin_loaded[b.par], b)
                if not (b.static and b.c < 2):
                    wait_half(dve, fin_stored[b.par], b.plus(-2))
                fo = fin_out[:, b.par, :].rearrange("p (t c) -> p t c", t=NT)
                V.tensor_tensor(fin_out[:, b.par, :], fin_in[:, b.par, 0, :], fin_in[:, b.par, 1, :], ALU.add).then_inc(fin_step.sem, 1)
                wait(dve, fin_step, b, 1)
                V.tensor_tensor(fo, fo, fin_gb[:, b.par, :].unsqueeze(1).to_broadcast([P, NT, DIM]), ALU.mult).then_inc(fin_step.sem, 1)
                wait(dve, fin_step, b, 2)
                V.tensor_tensor(fin_out[:, b.par, :], fin_out[:, b.par, :], xres[:, bass.ds(b.n * SEQ, SEQ)], ALU.add).then_inc(fin_step.sem, 1)

            for c in range(2):
                final(Batch(None, c))
            with dve.Fori(0, NB // 2 - 1) as pair:
                for c in range(2):
                    final(Batch(pair, c + 2))

        def ffn_pool(pool):
            def store(j):
                t_wait(pool, rows_ready, j)
                settle(pool)
                nc.gpsimd.indirect_dma_start(pair_out, bass.IndirectOffsetOnAxis(rows_in[:, j.slot, DIM:DIM + 1].bitcast(U32), 0),
                                             rows_out[:, j.slot, :], None, bounds_check=ROUTED - 1, oob_is_err=False
                                             ).then_inc(pairs_stored[j.slot], 16)

            for c in range(RING):
                store(Tile(None, c))
            with pool.Fori(1, FFN_TILES // RING) as reg:
                for c in range(RING):
                    store(Tile(reg, c))

        @block.sync
        def _(sp):
            for dst, src in ((idf[:], ident), (maskf, mask_q), (beforef, before), (iota8[:], iota),
                             (wqk[:], w_qk), (wv[:], w_v), (wo[:], w_o), (rmsc[:], rms_col), (rw[:], router_w),
                             (rb[:], router_b), (ct[:], c_t)):
                sp.dma_start(dst, src).then_inc(consts_loaded, 16)
            for j in range(4):
                sp.dma_start(lamv[:, j, :], lambdas[j]).then_inc(consts_loaded, 16)
            sp.dma_start(w_mod_sb, w_mod).then_inc(consts_loaded, 16)
            sp.dma_start(posm_ramp[:], ramp).then_inc(consts_loaded, 16)
            for dst, src in ((pairno, pair_no), (tileno, tile_no), (fill, filler)):
                sp.dma_start(dst[:], src).then_inc(consts_loaded, 16)
            sp.wait_ge(setup_v, SETUP_ROWS)
            sp.dma_start(mod_rows.rearrange("b (j c) -> b j c", j=4), mrow[:, :, :]).then_inc(mods_saved, 16)
            sp.wait_ge(mods_saved, 16)

            def body(i):
                b = i.plus(4)
                if active(b):
                    wait(sp, stats1, b.plus(-2), 1)
                    sp.dma_start(xres[:, bass.ds(b.n * SEQ, SEQ)].rearrange("p (t c) -> p t c", t=NT),
                                 x[bass.ds(b.n, 1)].rearrange("a (t p) c -> p (a t) c", p=P)
                                 ).then_inc(x_loaded[b.par].sem, 16)
                b = i.plus(1)
                if active(b):
                    load_unit(b, 1)
                b = i
                if active(b):
                    move_max(b, 1)
                b = i.plus(2)
                if active(b):
                    wait(sp, l_ready, b)
                    for s, part in enumerate(Q_SLOTS):
                        buf = (part_h, part_m, part_l)[part]
                        sp.dma_start(q_parts[bass.ds(b.n, 1), :, s, :, :, :].rearrange("a t d h k -> (a d h) t k"),
                                     buf[:, 0, :].rearrange("p (t k) -> p t k", t=2)
                                     ).then_inc(parts_saved.sem, 16)
                    for part, buf in enumerate((part_h, part_m, part_l)):
                        sp.dma_start(k_parts[bass.ds(b.n, 1), :, part, :, :, :].rearrange("a t d h k -> (a d h) t k"),
                                     buf[:, 1, :].rearrange("p (t k) -> p t k", t=2)
                                     ).then_inc(parts_saved.sem, 16)
                    wait(sp, parts_saved, b)
                    load_unit(b, 0)
                b = i.plus(1)
                if active(b):
                    move_max(b, 0)
                b = i.plus(-1)
                if active(b):
                    wait(sp, h2_step, b.plus(-2))
                    sp.dma_start(mods[:, b.par, :, :],
                                 mod_rows[bass.ds(b.n, 1), 0:3 * DIM].rearrange("a (j c) -> a j c", j=3)
                                 .to_broadcast([P, 3, DIM])).then_inc(mods_loaded[b.par].sem, 16)

            def load_unit(b, w):
                slot = 2 * b.par + w
                wait(sp, exp_ps, b.plus(-2), NBANKS // 2 * (w + 1))
                wait(sp, parts_saved, b)
                sp.dma_start(qt[0:QK_ROWS, slot, :, :],
                             q_parts[bass.ds(b.n, 1), :, :, :, w * HU:(w + 1) * HU, :]
                             .rearrange("a t s d h k -> (a t s d) h k")).then_inc(unit_loaded[w].sem, 16)
                for t in range(2):
                    for s0, ns in K_RUNS:
                        r0 = t * HALF_ROWS + s0 * DH
                        sp.dma_start(kt[r0:r0 + ns * DH, slot, t, :, :],
                                     k_parts[bass.ds(b.n, 1), t, 0:ns, :, w * HU:(w + 1) * HU, :]
                                     .rearrange("a s d h k -> (a s d) h k")).then_inc(unit_loaded[w].sem, 16)

            def move_max(b, w):
                wait(sp, nmt_ready, b, w + 1)
                sp.dma_start(max_parts[bass.ds(b.n, 1), w].rearrange("a r h k -> (a r h) k"),
                             nmt[:, w, :]).then_inc(nm_saved.sem, 16)
                wait(sp, nm_saved, b, 16 * (w + 1))
                sp.dma_start(qt[QK_ROWS:ALL_ROWS, 2 * b.par + w, :, :],
                             max_parts[bass.ds(b.n, 1), w].rearrange("a r h k -> (a r) h k")
                             ).then_inc(nm_loaded[w].sem, 16)

            iterations(sp, body)
            ffn_sp(sp)

        @block.tensor
        def _(pe):
            pe.wait_ge(setup_v, SETUP_SILU)
            for j in range(2):
                m = nc.tensor.matmul(p_mix[:, 0, j * NB:(j + 1) * NB], w_mod_sb[:, j * DIM:(j + 1) * DIM],
                                     silu_t[:, 2, :], start=True, stop=True)
            nc.tensor.matmul(p_max[0:NB, 0, 0:2 * DIM], silu_t[:, 2, :], w_mod_sb[:, 2 * DIM:4 * DIM], start=True, stop=True)
            m = nc.tensor.matmul(p_max[0:NB, 1, 0:2 * DIM], silu_t[:, 2, :], w_mod_sb[:, 4 * DIM:6 * DIM], start=True, stop=True)
            m.then_inc(setup_t, 1)
            pe.wait_ge(setup_v, SETUP_DONE)
            pe.wait_ge(setup_a, 2)

            def scores_for_max(b, h, n, rows):
                w, h8, bank = h // HU, h % HU, n % 2
                slot = 2 * b.par + w
                if n in (0, NBANKS // 2):
                    wait(pe, unit_loaded[w], b)
                if n >= 2:
                    wait(pe, max_done, b, n - 1)
                else:
                    wait(pe, max_done, b.plus(-1), NBANKS - 1 + n)
                if rows == 1:
                    for t in range(2):
                        nc.tensor.matmul(p_max[:, bank, t * SEQ:(t + 1) * SEQ], qt[0:QK_ROWS, slot, h8, P:SEQ],
                                         kt[0:QK_ROWS, slot, t, h8, :], start=(t == 0), stop=False)
                    m = nc.tensor.matmul(p_max[:, bank, :].rearrange("p (t k) -> p t k", t=2)[:, :, P:SEQ], idb[:],
                                         mask4[:, 0:2, :], start=False, stop=True)
                else:
                    for hh in range(2):
                        for t in range(2):
                            c = (2 * t + hh) * P
                            nc.tensor.matmul(p_max[:, bank, c:c + P], qt[0:QK_ROWS, slot, h8 - 1 + hh, 0:P],
                                             kt[0:QK_ROWS, slot, t, h8 - 1 + hh, 0:P],
                                             start=(t == 0 and hh == 0), stop=False)
                    m = nc.tensor.matmul(p_max[:, bank, :].rearrange("p (j k) -> p j k", j=4), idb[:], mask4[:],
                                         start=False, stop=True)
                m.then_inc(max_ps.sem, 1)

            def scores_for_exp(b, h, n, tile):
                w, h8, bank = h // HU, h % HU, n % 3
                slot = 2 * b.par + w
                if n in (0, NBANKS // 2):
                    wait(pe, nm_loaded[w], b)
                if n >= 3:
                    wait(pe, exp_done, b, n - 2)
                else:
                    wait(pe, exp_done, b.plus(-1), NBANKS - 2 + n)
                if tile == 0:
                    for t in range(2):
                        m = nc.tensor.matmul(p_exp[:, bank, t * SEQ:(t + 1) * SEQ], kt[0:ALL_ROWS, slot, t, h8, 0:P],
                                             qt[0:ALL_ROWS, slot, h8, :], start=True, stop=True)
                else:
                    for hh in range(2):
                        for t in range(2):
                            c = (2 * hh + t) * P
                            m = nc.tensor.matmul(p_exp[:, bank, c:c + P], kt[0:ALL_ROWS, slot, t, h8 - 1 + hh, P:SEQ],
                                                 qt[0:ALL_ROWS, slot, h8 - 1 + hh, P:SEQ], start=True, stop=True)
                m.then_inc(exp_ps.sem, 1)

            def outputs(b, g):
                if g == 0:
                    wait(pe, v_ready, b)
                wait(pe, masked, b, 3 * (g + 1))
                if g % 2 == 0:
                    wait(pe, ot_ready, b, g // 2) if g else wait(pe, ot_ready, b.plus(-1))
                for tile in range(NT):
                    n = SEQ if tile == 0 else P
                    for j in range(4):
                        src = (probs[:, g % 2, j // 2, (j % 2) * SEQ:(j % 2 + 1) * SEQ] if tile == 0
                               else probs[:, g % 2, 2, j * P:(j + 1) * P])
                        m = nc.tensor.matmul(p_out[32 * j:32 * j + 32, g % 2, SEQ - n:SEQ],
                                             v[:, b.par, tile, 2 * g + j // 2, :], src,
                                             start=(tile == 0), stop=(tile == 1))
                m.then_inc(pv_done.sem, 1)

            def outputs_to_rows(i, b, w, tile, bank, turn):
                mix_free(pe, i, bank, turn)
                wait(pe, ot_ready, b, 2 * (w + 1))
                for g in range(4):
                    m = nc.tensor.transpose(p_mix[:, bank, g * P:(g + 1) * P], ot[:, w, g, tile * P:(tile + 1) * P], idf[:])
                m.then_inc(ot_ps.sem, 1)

            def project(i, b, j, turn):
                mix_free(pe, i, 0, turn)
                for t in range(2):
                    m = nc.tensor.matmul(p_mix[:, 0, t * SEQ:(t + 1) * SEQ], wqk[:, 2 * j + t, :], ht[:, b.par, :],
                                         start=True, stop=True)
                m.then_inc(proj_ps.sem, 1)

            def max_to_rows(i, b, w, turn):
                mix_free(pe, i, 1, turn)
                wait(pe, nm_step, b, 4 * (w + 1))
                settle(pe)
                pm = p_mix[:, 1, 0:P].bitcast(BF16)
                for tile in range(NT):
                    m = nc.tensor.transpose(pm[0:MAX_ROWS * HU, tile * P:(tile + 1) * P],
                                            nm[:, w, 2 * tile:2 * tile + 2, :, :].rearrange("p t s h -> p (t s h)"), idb[:])
                m.then_inc(nm_ps.sem, 1)

            def body(i):
                bA, bV, b1, b2, bC, bW, bR = (i.plus(d) for d in (2, 1, 1, 0, -1, -2, -3))
                for s in range(NH):
                    n = s + s // 2
                    if active(b1):
                        scores_for_max(b1, s, n, 1)
                    if active(b2):
                        scores_for_exp(b2, s, n, 0)
                    if active(b1) and s % 2:
                        scores_for_max(b1, s, n + 1, 0)
                    if active(b2) and s % 2:
                        scores_for_exp(b2, s, n + 1, 1)
                    if s % 2:
                        g = s // 2 - 1
                        if g >= 0 and active(b2):
                            outputs(b2, g)
                        if g < 0 and active(bC):
                            outputs(bC, g + PAIRS)
                    if s == 0 and active(bA):
                        mix_free(pe, i, 0, 0)
                        wait(pe, xn_ready, bA)
                        for tile in range(NT):
                            m = nc.tensor.transpose(p_mix[:, 0, tile * P:(tile + 1) * P], xn[:, tile, :], idf[:])
                        m.then_inc(xt_ps.sem, 1)
                    if s == 0 and active(bW):
                        mix_free(pe, i, 1, 0)
                        wait(pe, on_ready, bW)
                        for half in range(2):
                            for tile in range(NT):
                                m = nc.tensor.transpose(
                                    p_mix[:, 1, (2 * half + tile) * P:(2 * half + tile + 1) * P],
                                    on_tok[:, tile, half * P:(half + 1) * P], idf[:])
                        m.then_inc(ont_ps.sem, 1)
                    if s == 1 and active(bA):
                        wait(pe, ht_ready, bA)
                        project(i, bA, 0, 1)
                    if s == 1 and active(bW):
                        mix_free(pe, i, 1, 1)
                        wait(pe, ont_ready, bW)
                        for tile in range(NT):
                            for half in range(2):
                                m = nc.tensor.matmul(p_mix[:, 1, tile * P:(tile + 1) * P],
                                                     ont[:, half, tile * P:(tile + 1) * P], wo[:, half, :],
                                                     start=(half == 0), stop=(half == 1))
                        m.then_inc(wo_ps.sem, 1)
                    if s == 3 and active(b2):
                        max_to_rows(i, b2, 1, 2)
                    if s == 3 and active(bA):
                        project(i, bA, 1, 2)
                    if s == 4 and active(bC):
                        outputs_to_rows(i, bC, 1, 0, 1, 3)
                    if s == 5 and active(bC):
                        outputs_to_rows(i, bC, 1, 1, 0, 3)
                    if s == 6 and active(bR):
                        mix_free(pe, i, 1, 4)
                        wait(pe, h2_step, bR)
                        for tile in range(NT):
                            m = nc.tensor.transpose(p_mix[:, 1, tile * P:(tile + 1) * P], h2[:, bR.par, 0, tile, 0:DIM], idf[:])
                        m.then_inc(h2t_ps.sem, 1)
                    if s == 7 and active(bR):
                        mix_free(pe, i, 1, 5)
                        wait(pe, h2t_ready, bR)
                        for tile in range(NT):
                            m = nc.tensor.matmul(p_mix[:, 1, tile * NE:(tile + 1) * NE], h2t[:, tile * P:(tile + 1) * P],
                                                 rw[:], start=True, stop=True)
                        m.then_inc(lg_ps.sem, 1)
                    if s == 8 and active(bV):
                        mix_free(pe, i, 0, 4)
                        wait(pe, ht_ready, bV)
                        for tile in range(NT):
                            m = nc.tensor.matmul(p_mix[:, 0, tile * SEQ:(tile + 1) * SEQ],
                                                 ht[:, bV.par, tile * P:(tile + 1) * P], wv[:], start=True, stop=True)
                        m.then_inc(v_ps.sem, 1)
                    if s == 9 and active(b1):
                        max_to_rows(i, b1, 0, 6)
                    if s == 10 and active(bR):
                        mix_free(pe, i, 1, 7)
                        wait(pe, route, bR, ROUTE_BOTH)
                        nc.tensor.matmul(p_mix[:, 1, 0:2 * NE], beforeb[:], both[:].rearrange("p t e -> p (t e)"),
                                         start=True, stop=False)
                        nc.tensor.matmul(p_mix[:, 1, NE:2 * NE], onesb[:], both[:, 0, :], start=False, stop=True)
                        for tile in range(NT):
                            m = nc.tensor.matmul(p_mix[:, 1, 2 * NE:3 * NE], onesb[:], both[:, tile, :],
                                                 start=(tile == 0), stop=(tile == NT - 1))
                        m.then_inc(rank_ps.sem, 1)
                    if s == 11 and active(b2):
                        outputs_to_rows(i, b2, 0, 0, 0, 5)
                    if s == 12 and active(b2):
                        outputs_to_rows(i, b2, 0, 1, 1, 8)

            iterations(pe, body)
            ffn_products(pe)

        @block.scalar
        def _(act):
            act.wait_ge(consts_loaded, 16 * CONSTS)
            nc.scalar.activation(silu_t[:, 0, :], ct[:], ACT.Exp, scale=-1.0).then_inc(setup_a, 1)
            act.wait_ge(setup_v, SETUP_LAM)
            nc.scalar.activation(lams[:], lams[:], ACT.Exp).then_inc(setup_a, 1)
            for dst, src in ((wg, gate_w), (wu, up_w), (wd, down_w)):
                act.dma_start(dst[:], src).then_inc(ffn_w_loaded, 16)
            act.wait_ge(setup_v, SETUP_DONE)

            def copy_outputs(b, q):
                wait(act, pv_done, b, 2 * (q + 1))
                wait(act, ot_ps, b.plus(-1), 2 * (q // 2 + 1))
                nc.scalar.copy(ot[:, q // 2, 2 * (q % 2):2 * (q % 2) + 2, :], p_out[:, :, :]).then_inc(ot_ready.sem, 1)

            def exp_bank(b, n):
                g, k = n // 3, n % 3
                wait(act, exp_ps, b, n + 1)
                if k == 0:
                    wait(act, pv_done, b, g - 1) if g >= 2 else wait(act, pv_done, b.plus(-1), PAIRS - 1 + g)
                nc.scalar.activation(probs[:, g % 2, k, :], p_exp[:, k, :], ACT.Exp, scale=SCALE).then_inc(exp_done.sem, 1)

            def copy_max(b, w):
                wait(act, nm_ps, b, w + 1)
                wait(act, nm_saved, b.plus(-1), 16 * (w + 1))
                pm = p_mix[:, 1, 0:P].bitcast(BF16)
                nc.scalar.copy(nmt[:, w, :], pm[0:MAX_ROWS * HU, :]).then_inc(nmt_ready.sem, 1)

            def high_part(b, j):
                wait(act, proj_ps, b, j + 1)
                wait(act, parts_saved, b.plus(-1))
                nc.scalar.copy(part_h[:, j, :], p_mix[:, 0, :]).then_inc(h_ready.sem, 1)

            def middle_part(b, j):
                wait(act, r_ready, b, j + 1)
                nc.scalar.copy(part_m[:, j, :], rest[:, j, :]).then_inc(m_ready.sem, 1)

            def body(i):
                bA, bV, b1, b2, bC, bW, bR = (i.plus(d) for d in (2, 1, 1, 0, -1, -2, -3))
                for s in range(NH):
                    if active(b2):
                        exp_bank(b2, s + s // 2)
                        if s % 2:
                            exp_bank(b2, s + s // 2 + 1)
                    if s == 0 and active(bA):
                        wait(act, xt_ps, bA)
                        wait(act, v_ps, bA.plus(-2))
                        nc.scalar.activation(ht[:, bA.par, :], p_mix[:, 0, 0:SEQ], ACT.Identity,
                                             bias=sa_t[:, bass.ds(bA.n, 1)], scale=ca_t[:, bass.ds(bA.n, 1)]
                                             ).then_inc(ht_ready.sem, 1)
                    if s == 0 and active(bW):
                        wait(act, ont_ps, bW)
                        nc.scalar.copy(ont[:].rearrange("p a k -> p (a k)"), p_mix[:, 1, :]).then_inc(ont_ready.sem, 1)
                    if s in (6, 10, 14) and active(b2):
                        copy_outputs(b2, (s - 6) // 4)
                    if s == 2 and active(bC):
                        copy_outputs(bC, 3)
                    if s == 1 and active(bA):
                        high_part(bA, 0)
                    if s == 3 and active(bA):
                        middle_part(bA, 0)
                    if s == 3 and active(b2):
                        copy_max(b2, 1)
                    if s == 3 and active(bA):
                        high_part(bA, 1)
                    if s == 5 and active(bA):
                        middle_part(bA, 1)
                    if s == 6 and active(bR):
                        wait(act, h2t_ps, bR)
                        nc.scalar.copy(h2t[:], p_mix[:, 1, 0:SEQ]).then_inc(h2t_ready.sem, 1)
                    if s == 7 and active(bR):
                        wait(act, h2_step, bR)
                        nc.scalar.copy(h2[:, bR.par, 1, :, 0:DIM], h2[:, bR.par, 0, :, 0:DIM]).then_inc(h2_copied.sem, 1)
                    if s == 8 and active(bV):
                        wait(act, v_ps, bV)
                        wait(act, pv_done, bV.plus(-2))
                        nc.scalar.copy(v[:, bV.par, :, :, 0:2 * DH].rearrange("p t h d -> p (t h) d"),
                                       p_mix[:, 0, :].rearrange("p (j d) -> p j d", d=2 * DH)).then_inc(v_ready.sem, 1)
                    if s == 9 and active(b1):
                        copy_max(b1, 0)
                    if s == 10 and active(bR):
                        wait(act, route, bR, ROUTE_DIFF)
                        nc.scalar.activation(gexp[:], gdiff[:], ACT.Exp).then_inc(gexp_ready.sem, 1)

            iterations(act, body)
            ffn_activations(act)

        @block.vector
        def _(dve):
            count = [0]

            def step(ins):
                count[0] += 1
                ins.then_inc(setup_v, 1)
                dve.wait_ge(setup_v, count[0])

            V = nc.vector
            V.memset(kt[:].rearrange("p a t h k -> p (a t h k)").bitcast(U32), 0)
            V.memset(v[:], 0.0)
            V.memset(onesb[:], 1.0)
            V.memset(rstd[:], 1.0)
            V.memset(rms_ss[:], 1.0)
            V.memset(mv1[:], 1.0)
            V.memset(mv2[:], 1.0)
            step(V.memset(var[:], 1.0))
            V.memset(v[:, :, :, :, 2 * DH:2 * DH + 1], 1.0)
            V.memset(kt[QK_ROWS:QK_ROWS + 3, :, 0, :, :], 1.0)
            step(V.memset(kt[QK_ROWS:ALL_ROWS, :, 1, :, :], 1.0))
            step(V.memset(kt[QK_ROWS:QK_ROWS + 3, :, 1, :, :], 0.0))
            dve.wait_ge(consts_loaded, 16 * CONSTS)
            V.tensor_copy(idb[:], idf[:])
            V.tensor_copy(beforeb[:], beforef)
            for j in range(4):
                V.tensor_copy(mask4[:, j, :], maskf)
            V.tensor_copy(carry[:], posm_ramp[:])
            step(V.tensor_scalar(wo[:], wo[:], rmsc[:, 0:1], 1.0 - LAMBDA_INIT, ALU.mult, ALU.mult))
            for j in range(2):
                last = V.tensor_tensor(lamv[:, 2 * j, :], lamv[:, 2 * j, :], lamv[:, 2 * j + 1, :], ALU.mult)
            step(last)
            for j in range(2):
                last = V.reduce_sum(lams[:, j, :], lamv[:, 2 * j, :].rearrange("p (h d) -> p h d", d=DH), AX.X)
            step(last)
            assert count[0] == SETUP_LAM
            dve.wait_ge(setup_a, 1)
            step(V.tensor_scalar(silu_t[:, 0, :], silu_t[:, 0, :], 1.0, None, ALU.add))
            step(V.reciprocal(silu_t[:, 1, :], silu_t[:, 0, :]))
            step(V.tensor_tensor(silu_t[:, 2, :], silu_t[:, 1, :], ct[:], ALU.mult))
            assert count[0] == SETUP_SILU
            dve.wait_ge(setup_t, 1)
            V.tensor_copy(sa_t[:], p_mix[:, 0, 0:NB])
            V.tensor_scalar(ca_t[:], p_mix[:, 0, NB:2 * NB], 1.0, None, ALU.add)
            V.tensor_scalar(mrow[:, 1, :], p_max[0:NB, 1, 0:DIM], 1.0, None, ALU.add)
            V.tensor_copy(mrow[:, 2, :], p_max[0:NB, 0, DIM:2 * DIM])
            for dst, src in ((0, p_max[0:NB, 0, 0:DIM]), (3, p_max[0:NB, 1, DIM:2 * DIM])):
                step(V.tensor_scalar(mtmp[:, 0, :], src, -1.0, 0.25, ALU.mult, ALU.max))
                step(V.tensor_tensor(mtmp[:, 0, :], mtmp[:, 0, :], src, ALU.max))
                step(V.tensor_scalar(mtmp[:, 1, :], src, 0.0, 2.0, ALU.is_ge, ALU.mult))
                step(V.tensor_scalar(mtmp[:, 1, :], mtmp[:, 1, :], -1.0, None, ALU.add))
                step(V.tensor_tensor(mrow[:, dst, :], mtmp[:, 0, :], mtmp[:, 1, :], ALU.mult))
            assert count[0] == SETUP_ROWS
            dve.wait_ge(setup_a, 2)
            step(V.tensor_tensor(neg_lam[:], lams[:, 1, :], lams[:, 0, :], ALU.subtract))
            step(V.tensor_scalar(neg_lam[:], neg_lam[:], -LAMBDA_INIT, None, ALU.add))
            assert count[0] == SETUP_DONE

            def take_max(b, h, n, rows):
                w, h8, bank = h // HU, h % HU, n % 2
                wait(dve, max_ps, b, n + 1)
                if n in (0, NBANKS // 2):
                    wait(dve, nm_step, b.plus(-1), 4 * (w + 1))
                if rows == 1:
                    m = V.reduce_max(mx[:, w, 1, :, h8:h8 + 1].rearrange("p t o -> p (t o)"),
                                     p_max[:, bank, :].rearrange("p (t k) -> p t k", t=2), AX.X)
                else:
                    m = V.reduce_max(mx[:, w, 0, :, h8 - 1:h8 + 1],
                                     p_max[:, bank, :].rearrange("p (t h k) -> p t h k", t=2, h=2), AX.X)
                m.then_inc(max_done.sem, 1)

            def minus_max(b, w, k):
                src = mx[:, w].rearrange("p a t h -> p (a t) h")
                if k == 0:
                    wait(dve, max_done, b, NBANKS // 2 * (w + 1))
                    wait(dve, nm_ps, b.plus(-1), w + 1)
                    ins = V.tensor_scalar(nm[:, w, :, 0, :], src, -1.0, None, ALU.mult)
                else:
                    wait(dve, nm_step, b, 4 * w + k)
                if k == 1:
                    ins = V.scalar_tensor_tensor(mrest[:], src, -1.0, nm[:, w, :, 0, :], ALU.mult, ALU.subtract)
                if k == 2:
                    ins = V.tensor_copy(nm[:, w, :, 1, :], mrest[:])
                if k == 3:
                    ins = V.tensor_tensor(nm[:, w, :, 2, :], mrest[:], nm[:, w, :, 1, :], ALU.subtract)
                ins.then_inc(nm_step.sem, 1)

            def rest_part(b, j):
                wait(dve, h_ready, b, j + 1)
                wait(dve, l_ready, b.plus(-1), j + 1)
                V.tensor_tensor(rest[:, j, :], p_mix[:, 0, :], part_h[:, j, :], ALU.subtract).then_inc(r_ready.sem, 1)

            def normalise(b, w, tile, bank, k):
                n = 2 * w + tile
                src = p_mix[:, bank, :].rearrange("p (h t d) -> p h t d", t=2, d=VW)
                r3 = rec[:].rearrange("p (h t) -> p h t", t=2)
                if k == 0:
                    wait(dve, ot_ps, b, n + 1)
                    wait(dve, on2_ready, b, n) if n else wait(dve, on2_ready, b.plus(-1))
                    V.reciprocal(r3, src[:, :, :, 2 * DH]).then_inc(rec_step.sem, 1)
                if k == 1:
                    wait(dve, rec_step, b, 2 * n + 1)
                    V.tensor_tensor(r3[:, :, 1], r3[:, :, 1], neg_lam[:, w * HU:(w + 1) * HU], ALU.mult).then_inc(rec_step.sem, 1)
                if k == 2:
                    wait(dve, rec_step, b, 2 * n + 2)
                    wait(dve, o_ready, b.plus(-1))
                    V.tensor_tensor(on2[:, tile, w * HU:(w + 1) * HU].rearrange("p h t d -> p (h t) d"),
                                    p_mix[:, bank, :].rearrange("p (j d) -> p j d", d=VW)[:, :, 0:2 * DH],
                                    rec[:].unsqueeze(2).to_broadcast([P, 2 * HU, 2 * DH]), ALU.mult).then_inc(on2_ready.sem, 1)

            def statistics(b, which, event):
                for tile in range(NT):
                    V.bn_stats(stats[:, which, tile, :], xres[:, bass.ds(b.n * SEQ + tile * DIM, DIM)]).then_inc(event.sem, 1)

            def mean_and_variance(b, which, event, mv, tile):
                wait(dve, event, b, tile + 1)
                settle(dve)
                V.bn_aggr(mv[:, tile, :], stats[:, which, tile, :]).then_inc(event.sem, 1)

            def inverse_roots(i, steps):
                bL, bC, bW = (i.plus(d) for d in (3, -1, -2))
                done = NEWTON * (i.n + LEAD)
                for k in steps:
                    if not i.static or done + k > 0:
                        dve.wait_ge(newton, done + k)
                    if k == 0:
                        if active(bC):
                            wait(dve, rms_sum, bC)
                        if active(bL):
                            wait(dve, stats1, bL)
                        if active(bW):
                            wait(dve, stats2, bW)
                        V.tensor_scalar(var[:, 0:NT * NH], rms_ss[:], 1.0 / (2 * DH), EPS, ALU.mult, ALU.add)
                        V.tensor_scalar(var[:, NT * NH:NT * NH + NT], mv1[:, :, 1], EPS, None, ALU.add)
                        ins = V.tensor_scalar(var[:, NT * NH + NT:NV], mv2[:, :, 1], EPS, None, ALU.add)
                    elif k == 1:
                        ins = V.tensor_scalar(nt1[:].bitcast(I32), var[:].bitcast(I32), 1, None, ALU.logical_shift_right)
                    elif k == 2:
                        if active(bC.plus(-1)):
                            wait(dve, on_ready, bC.plus(-1))
                        if active(bL.plus(-1)):
                            wait(dve, xn_ready, bL.plus(-1))
                        if active(bW.plus(-1)):
                            wait(dve, xn2_ready, bW.plus(-1))
                        ins = V.tensor_scalar(rstd[:].bitcast(I32), nt1[:].bitcast(I32), -1.0, float(0x5F3759DF), ALU.mult, ALU.add)
                    elif k % 3 == 0:
                        ins = V.tensor_tensor(nt1[:], rstd[:], rstd[:], ALU.mult)
                    elif k % 3 == 1:
                        ins = V.scalar_tensor_tensor(nt2[:], nt1[:], -0.5, var[:], ALU.mult, ALU.mult)
                    else:
                        ins = V.scalar_tensor_tensor(rstd[:], nt2[:], 1.5, rstd[:], ALU.add, ALU.mult)
                    ins.then_inc(newton, 1)

            def body(i):
                bL, bA, bV, b1, b2, bC, bW, bR = (i.plus(d) for d in (3, 2, 1, 1, 0, -1, -2, -3))
                for s in range(NH):
                    n = s + s // 2
                    if active(b1):
                        take_max(b1, s, n, 1)
                    if s < 2 and active(b2):
                        minus_max(b2, 1, s)
                    if s == 2 and active(b2):
                        minus_max(b2, 1, 3)
                    if s == 2 and active(bA):
                        rest_part(bA, 0)
                    if s == 2 and active(bW):
                        wait(dve, wo_ps, bW)
                        wait_half(dve, mods_loaded[bW.par], bW)
                        V.tensor_tensor(xtmp[:], p_mix[:, 1, 0:SEQ].rearrange("p (t c) -> p t c", t=NT),
                                        mods[:, bW.par, 0:1, :].to_broadcast([P, NT, DIM]), ALU.mult).then_inc(attn_scaled.sem, 1)
                    if s == 3 and active(bW):
                        wait(dve, attn_scaled, bW)
                        xb = xres[:, bass.ds(bW.n * SEQ, SEQ)]
                        V.tensor_tensor(xb, xb, xtmp[:].rearrange("p t c -> p (t c)"), ALU.add).then_inc(x1_ready.sem, 1)
                    if s == 4 and active(bA):
                        rest_part(bA, 1)
                    if s == 4 and active(bW):
                        wait(dve, x1_ready, bW)
                        settle(dve)
                        statistics(bW, 1, stats2)
                    if s == 5:
                        for k in range(3):
                            if active(bC):
                                normalise(bC, 1, 0, 1, k)
                            if k < NT and active(bW):
                                mean_and_variance(bW, 1, stats2, mv2, k)
                    if s == 6 and active(bC):
                        for k in range(3):
                            normalise(bC, 1, 1, 0, k)
                    if s == 8:
                        if active(bR):
                            wait(dve, route, bR.plus(-1))
                            wait(dve, lg_ps, bR)
                            V.tensor_tensor(lg[:], p_mix[:, 1, 0:NT * NE].rearrange("p (t e) -> p t e", t=NT),
                                            rb[:].unsqueeze(1).to_broadcast([P, NT, NE]), ALU.add).then_inc(route.sem, 1)
                        if active(b1):
                            minus_max(b1, 0, 0)
                        if active(bR):
                            wait(dve, route, bR, 1)
                            settle(dve)
                            for tile in range(NT):
                                V.max(top8[:, tile, :], lg[:, tile, :]).then_inc(route.sem, 1)
                        if active(b1):
                            minus_max(b1, 0, 1)
                        if active(bR):
                            wait(dve, route, bR, 3)
                            settle(dve)
                            for tile in range(NT):
                                V.max_index(top8i[:, tile, :], top8[:, tile, :], lg[:, tile, :]).then_inc(route.sem, 1)
                            V.tensor_tensor(gdiff[:], top8[:, :, 1], top8[:, :, 0], ALU.subtract).then_inc(route.sem, 1)
                        if active(b1):
                            minus_max(b1, 0, 2)
                        if active(bR):
                            wait(dve, route, bR, 5)
                            V.tensor_copy(topf[:].rearrange("p j t -> p t j"), top8i[:, :, 0:2]).then_inc(route.sem, 1)
                        if active(b1):
                            minus_max(b1, 0, 3)
                        if active(bR):
                            wait(dve, route, bR, 7)
                            V.tensor_tensor(chosen[:], iota8[:].unsqueeze(1).to_broadcast([P, 2 * NT, NE]),
                                            topf[:].rearrange("p j t -> p (j t)").unsqueeze(2).to_broadcast([P, 2 * NT, NE]),
                                            ALU.is_equal).then_inc(route.sem, 1)
                    if s == 9 and active(bR):
                        wait(dve, route, bR, 8)
                        V.tensor_tensor(both[:], chosen[:, 0:NT, :], chosen[:, NT:2 * NT, :], ALU.add).then_inc(route.sem, 1)
                    if s == 9 and active(bL):
                        wait_half(dve, x_loaded[bL.par], bL)
                        settle(dve)
                        statistics(bL, 0, stats1)
                    if s == 10 and active(bC):
                        wait(dve, osq_ready, bC)
                        V.reduce_sum(rms_ss[:], osq[:], AX.X).then_inc(rms_sum.sem, 1)
                    if s == 11:
                        inverse_roots(i, [0])
                        if active(bR):
                            wait(dve, rank_ps, bR)
                            V.tensor_tensor(pos[:], p_mix[:, 1, 0:NT * NE].rearrange("p (t e) -> p t e", t=NT),
                                            carry[:].unsqueeze(1).to_broadcast([P, NT, NE]), ALU.add).then_inc(route.sem, 1)
                            wait(dve, gexp_ready, bR)
                            V.tensor_scalar(gden[:], gexp[:], 1.0, None, ALU.add).then_inc(route.sem, 1)
                        inverse_roots(i, [1])
                        if active(bR):
                            wait(dve, route, bR, 10)
                            V.tensor_tensor(carry[:], carry[:], p_mix[:, 1, 2 * NE:3 * NE], ALU.add).then_inc(route.sem, 1)
                            for j in range(2):
                                ins = V.tensor_tensor(posm[:, j * NT:(j + 1) * NT, :], chosen[:, j * NT:(j + 1) * NT, :], pos[:], ALU.mult)
                            ins.then_inc(route.sem, 1)
                        inverse_roots(i, [2])
                    if s == 12:
                        inverse_roots(i, [3])
                        hrow = h2[:, bR.par].rearrange("p j t r -> p (j t) r")
                        if active(b2):
                            normalise(b2, 0, 0, 0, 0)
                        if active(bR):
                            wait(dve, route, bR, 11)
                            V.reciprocal(hrow[:, 0:NT, DIM + 1], gden[:]).then_inc(route.sem, 1)
                        inverse_roots(i, [4])
                        if active(b2):
                            normalise(b2, 0, 0, 0, 1)
                        if active(bR):
                            wait(dve, route, bR, 13)
                            V.reduce_sum(posf[:], posm[:], AX.X).then_inc(route.sem, 1)
                        inverse_roots(i, [5])
                        if active(b2):
                            normalise(b2, 0, 0, 0, 2)
                        if active(bR):
                            wait(dve, route, bR, 14)
                            V.tensor_tensor(hrow[:, NT:2 * NT, DIM + 1], hrow[:, 0:NT, DIM + 1], gexp[:], ALU.mult)
                            V.tensor_copy(hrow[:, :, DIM].bitcast(I32), pairno[:])
                            wait(dve, route, bR, 15)
                            V.tensor_copy(idx[:, bR.par, :], posf[:]).then_inc(route.sem, 1)
                        inverse_roots(i, [6])
                    if s == 13:
                        inverse_roots(i, [7])
                        if active(b2):
                            normalise(b2, 0, 1, 1, 0)
                        inverse_roots(i, [8])
                        if active(b2):
                            normalise(b2, 0, 1, 1, 1)
                        if active(bR):
                            wait(dve, route, bR, ROUTE_ROWS)
                            V.tensor_scalar(pairno[:], pairno[:], float(SEQ), None, ALU.add).then_inc(route.sem, 1)
                        inverse_roots(i, [9])
                        if active(b2):
                            normalise(b2, 0, 1, 1, 2)
                    if s == 14:
                        inverse_roots(i, [10, 11])
                        dve.wait_ge(newton, NEWTON * (i.n + LEAD + 1))
                        if active(bL):
                            wait(dve, xt_ps, bL.plus(-1))
                            for tile in range(NT):
                                c = NT * NH + tile
                                V.tensor_scalar(xn[:, tile, :], xres[:, bass.ds(bL.n * SEQ + tile * DIM, DIM)],
                                                mv1[:, tile, 0:1], rstd[:, c:c + 1], ALU.subtract, ALU.mult).then_inc(xn_ready.sem, 1)
                        if active(bC):
                            wait(dve, ont_ps, bC.plus(-1))
                            V.tensor_tensor(on_tok[:].rearrange("p t (h d) -> p (t h) d", d=2 * DH), o[:],
                                            rstd[:, 0:NT * NH].unsqueeze(2).to_broadcast([P, NT * NH, 2 * DH]),
                                            ALU.mult).then_inc(on_ready.sem, 1)
                    if s == 15 and active(bW):
                        if not (bW.static and bW.c < 2):
                            wait_half(dve, scattered[bW.par], bW.plus(-2))
                        wait(dve, h2t_ps, bW.plus(-2))
                        for tile in range(NT):
                            c = NT * NH + NT + tile
                            V.tensor_scalar(h2[:, bW.par, 0, tile, 0:DIM], xres[:, bass.ds(bW.n * SEQ + tile * DIM, DIM)],
                                            mv2[:, tile, 0:1], rstd[:, c:c + 1], ALU.subtract, ALU.mult).then_inc(xn2_ready.sem, 1)
                    if active(b1) and s % 2:
                        take_max(b1, s, n + 1, 0)
                    if s == 1 and active(b2):
                        minus_max(b2, 1, 2)
                    if s == 9 and active(bL):
                        for tile in range(NT):
                            mean_and_variance(bL, 0, stats1, mv1, tile)

            iterations(dve, body)
            ffn_vector(dve)

        @block.gpsimd
        def _(pool):
            G = nc.gpsimd
            zero = G.to_reg(0.0)

            def mask_bank(b, n):
                g, k = n // 3, n % 3
                wait(pool, exp_done, b, n + 1)
                settle(pool)
                blocks = (probs[:, g % 2, k, :].rearrange("p (t k) -> p t k", t=2)[:, :, 0:P] if k < 2
                          else probs[:, g % 2, k, :].rearrange("p (t k) -> p t k", t=4))
                G.affine_select(out=blocks, in_=blocks, compare_op=ALU.is_ge, fill=zero, base=0,
                                pattern=[[0, 2 if k < 2 else 4], [1, P]], channel_multiplier=-1).then_inc(masked.sem, 1)

            def low_part(b, j):
                wait(pool, m_ready, b, j + 1)
                wait(pool, parts_saved, b.plus(-1))
                G.tensor_tensor(part_l[:, j, :], rest[:, j, :], part_m[:, j, :], ALU.subtract).then_inc(l_ready.sem, 1)

            def body(i):
                bA, b2, bC, bW, bR = (i.plus(d) for d in (2, 0, -1, -2, -3))
                for s in range(NH):
                    if active(b2):
                        mask_bank(b2, s + s // 2)
                        if s % 2:
                            mask_bank(b2, s + s // 2 + 1)
                    if s in (4, 6) and active(bA):
                        low_part(bA, (s - 4) // 2)
                    if s == 0 and active(bR):
                        wait(pool, xn2_ready, bR)
                        wait_half(pool, mods_loaded[bR.par], bR)
                        hb = h2[:, bR.par, 0, :, 0:DIM]
                        G.tensor_tensor(hb, hb, mods[:, bR.par, 1:2, :].to_broadcast([P, NT, DIM]), ALU.mult).then_inc(h2_step.sem, 1)
                    if s == 2 and active(bR):
                        wait(pool, h2_step, bR, 1)
                        hb = h2[:, bR.par, 0, :, 0:DIM]
                        G.tensor_tensor(hb, hb, mods[:, bR.par, 2:3, :].to_broadcast([P, NT, DIM]), ALU.add).then_inc(h2_step.sem, 1)
                    if s == 7 and active(bC):
                        wait(pool, on2_ready, bC)
                        wait(pool, on_ready, bC.plus(-1))
                        a = on2[:].rearrange("p a h t d -> p (a h) t d")
                        G.tensor_tensor(o[:], a[:, :, 0, :], a[:, :, 1, :], ALU.add).then_inc(o_ready.sem, 1)
                    if s == 8 and active(bC):
                        wait(pool, o_ready, bC)
                        wait(pool, rms_sum, bC.plus(-1))
                        G.tensor_tensor(osq[:], o[:], o[:], ALU.mult).then_inc(osq_ready.sem, 1)
                    if s in (12, 13, 14, 15) and active(bR):
                        k = s - 12
                        if k == 0:
                            wait(pool, route, bR, ROUTE_ROWS)
                            wait(pool, h2_copied, bR)
                            settle(pool)
                        G.indirect_dma_start(rows_sorted, bass.IndirectOffsetOnAxis(idx[:, bR.par, k:k + 1].bitcast(U32), 0),
                                             h2[:, bR.par, k // NT, k % NT, :], None).then_inc(scattered[bR.par].sem, 16)

            iterations(pool, body)
            ffn_pool(pool)


def kernel(L0_attn_X, L0_attn_W_q, L0_attn_W_k, L0_attn_W_v, L0_attn_W_o, L0_attn_lambda_q1, L0_attn_lambda_k1,
           L0_attn_lambda_q2, L0_attn_lambda_k2, L0_attn_rms_scale, L0_ffn_router_w, L0_ffn_router_b, L0_ffn_gate_w,
           L0_ffn_up_w, L0_ffn_down_w, L0_c, L0_wmod):
    import concourse.bacc as bacc
    from concourse.bass_utils import run_bass_kernel_spmd

    def lay(a):
        return np.ascontiguousarray(np.asarray(a))

    def halves(w):
        return lay(w).reshape(NH, 2, DH, DIM).transpose(3, 1, 2, 0).reshape(DIM, 2, DH * NH)

    def up_layout(w):
        return lay(w).transpose(2, 0, 1).reshape(DIM, NE * FF)

    p = np.arange(P)
    fill_row = np.zeros((P, RW), np.float32)
    fill_row[:, DIM] = np.full(P, SKIPPED, np.int32).view(np.float32)
    arrays = {
        "x": lay(L0_attn_X),
        "w_qk": lay(np.concatenate([halves(L0_attn_W_q), halves(L0_attn_W_k)], axis=1)),
        "w_v": lay(lay(L0_attn_W_v).T),
        "w_o": lay(lay(L0_attn_W_o).T.reshape(2, P, DIM).transpose(1, 0, 2)),
        "lambdas": lay(np.stack([np.broadcast_to(lay(a).reshape(-1), (P, NH * DH)) for a in
                                 (L0_attn_lambda_q1, L0_attn_lambda_k1, L0_attn_lambda_q2, L0_attn_lambda_k2)])),
        "rms_col": lay(np.tile(lay(L0_attn_rms_scale), P // (2 * DH)).reshape(P, 1)),
        "router_w": lay(lay(L0_ffn_router_w).T),
        "router_b": lay(np.broadcast_to(lay(L0_ffn_router_b), (P, NE))),
        "gate_w": lay(up_layout(L0_ffn_gate_w)),
        "up_w": lay(up_layout(L0_ffn_up_w)),
        "down_w": lay(lay(L0_ffn_down_w).reshape(NE, DIM, FCH, P).transpose(3, 0, 2, 1).reshape(P, NE * FF)),
        "c_t": lay(lay(L0_c).T),
        "w_mod": lay(L0_wmod),
        "ident": np.eye(P, dtype=np.float32),
        "mask_q": np.where(p[None, :] <= p[:, None], 0.0, NEG).astype(np.float32),
        "before": (p[:, None] < p[None, :]).astype(np.float32),
        "iota": lay(np.broadcast_to(np.arange(NE, dtype=np.float32), (P, NE))),
        "ramp": lay(np.broadcast_to(np.arange(NE, dtype=np.float32) * REGION, (P, NE))),
        "pair_no": (p[:, None] + np.array([[j * NB * SEQ + t * P for j in range(2) for t in range(NT)]])).astype(np.float32),
        "tile_no": lay(np.broadcast_to(np.arange(FFN_TILES, dtype=np.float32), (P, FFN_TILES))),
        "filler": fill_row,
    }
    nc = bacc.Bacc("TRN2", target_bir_lowering=False, num_devices=1)
    args = {n: nc.dram_tensor(f"in_{n}", a.shape, mybir.dt.from_np(a.dtype), kind="ExternalInput").ap()
            for n, a in arrays.items()}
    out = nc.dram_tensor("out_dram", (NB, SEQ, DIM), F32, kind="ExternalOutput").ap()
    adaln_block(nc, out=out, **args)
    r = run_bass_kernel_spmd(nc, [{f"in_{n}": a for n, a in arrays.items()}], core_ids=[0])
    return r.results[0]["out_dram"]
```

```python
import concourse.bass as bass
from concourse import mybir
from contextlib import ExitStack
import numpy as np

F32 = mybir.dt.float32
F32R = mybir.dt.float32r
BF16 = mybir.dt.bfloat16
I32 = mybir.dt.int32
U32 = mybir.dt.uint32
ALU = mybir.AluOpType
ACT = mybir.ActivationFunctionType
AX = mybir.AxisListType

P = 128
NB, SEQ, DIM = 32, 256, 128
NH, DH = 16, 8
NT = SEQ // P
NE, FF = 8, 512
FCH = FF // P
TILES = NB * NT
HU = NH // 2
EPS = 1e-5
LAMBDA_INIT = 0.8
SCALE = DH ** -0.5
NEG = -1e30
SLOTS = 6
HALF_ROWS = SLOTS * DH
QK_ROWS = 2 * HALF_ROWS
MAX_ROWS = 2 * 3
ALL_ROWS = QK_ROWS + MAX_ROWS
Q_SLOTS = (0, 0, 0, 1, 1, 2)
K_RUNS = ((0, 3), (3, 2), (5, 1))
VW = 32
ROUTED = 2 * NB * SEQ
REGION = NB * SEQ + P
RING = 8
GROUP, FIN_RING = 2, 4
FFN_TILES = -(-(ROUTED // P + NE - 1) // RING) * RING
LAST_PADS = FFN_TILES - ROUTED // P + 1
SORTED_ROWS = NE * REGION + LAST_PADS * P
RW = DIM + 2
SKIPPED = 1 << 20

BANK = 512
PAIRS = NH // 2
NBANKS = 3 * PAIRS
SETUP_SILU, SETUP_LAM, SETUP_ROWS, SETUP_DONE = 3, 5, 16, 18
ROUTE_DIFF, ROUTE_BOTH, ROUTE_CARRY, ROUTE_ROWS, ROUTE_STEPS = 6, 9, 12, 16, 17
NEWTON = 13


class Batch:

    def __init__(self, pair, c):
        self.pair_reg, self.c = pair, c
        self.static = pair is None
        self.n = c if pair is None else pair * 2 + c
        self.par = c % 2
        self.half = c // 2 if pair is None else pair + c // 2

    def plus(self, d):
        return Batch(self.pair_reg, self.c + d)


class Event:

    def __init__(self, sem, per=1):
        self.sem, self.per = sem, per

    def at(self, b, k=None):
        return b.n * self.per + (self.per if k is None else k)


def wait(eng, event, b, k=None):
    if b.static and (b.c < 0 or event.at(b, k) <= 0):
        return
    assert b.c * event.per + (event.per if k is None else k) > 0
    eng.wait_ge(event.sem, event.at(b, k))


def wait_half(eng, event, b):
    if b.static and b.c < 0:
        return
    assert b.c >= 0
    eng.wait_ge(event.sem, (b.half + 1) * event.per)


def adaln_block(nc, x, w_qk, w_v, w_o, lambdas, rms_col, router_w, router_b, gate_w, up_w, down_w,
                c_t, w_mod, max_ones, ident, mask_q, before, iota, ramp, pair_no, tile_no, filler, out):
    ctx = ExitStack()
    with ctx:
        def sb(name, shape, dt=F32):
            return ctx.enter_context(nc.sbuf_tensor(name, shape, dt))

        def ps(name, shape, dt=F32):
            return ctx.enter_context(nc.psum_tensor(name, shape, dt))

        def sem(name):
            return ctx.enter_context(nc.semaphore(name))

        def ev(name, per=1):
            return Event(sem(name), per)

        def dram(name, shape, dt=F32):
            return nc.dram_tensor(name, shape, dt, kind="Internal").ap()

        q_parts = dram("q_parts", [NB, 2, SLOTS, DH, NH, SEQ], BF16)
        k_parts = dram("k_parts", [NB, 2, 3, DH, NH, SEQ], BF16)
        max_parts = dram("max_parts", [NB, 2, MAX_ROWS, HU, SEQ], BF16)
        mod_rows = dram("mod_rows", [NB, 4 * DIM])
        rows_sorted = dram("rows_sorted", [SORTED_ROWS, RW])
        pair_out = dram("pair_out", [ROUTED, DIM])

        idf = sb("idf", [P, P])
        idb = sb("idb", [P, P], BF16)
        mask4 = sb("mask4", [P, 4, P], BF16)
        beforeb = sb("beforeb", [P, P], BF16)
        onesb = sb("onesb", [P, P], BF16)
        iota8 = sb("iota8", [P, NE])
        wqk = sb("wqk", [P, 4, P])
        wv = sb("wv", [P, NH * 2 * DH])
        wo = sb("wo", [P, 2, DIM])
        rmsc = sb("rmsc", [P, 1])
        rw = sb("rw", [P, NE])
        rb = sb("rb", [P, NE])
        lams = sb("lams", [P, 2, NH])
        neg_lam = sb("neg_lam", [P, NH])
        ct = sb("ct", [P, NB])
        silu_t = sb("silu_t", [P, 3, NB])
        sa_t = sb("sa_t", [P, NB])
        ca_t = sb("ca_t", [P, NB])
        mrow = sb("mrow", [NB, 4, DIM])
        wg = sb("wg", [P, NE * FF])
        wu = sb("wu", [P, NE * FF])
        wd = sb("wd", [P, NE * FF])

        xres = sb("xres", [P, TILES * DIM])

        qt = sb("qt", [P, 4, HU, SEQ], BF16)
        kt = sb("kt", [P, 4, 2, HU, SEQ], BF16)
        probs = sb("probs", [P, 2, 3, BANK])
        v = sb("v", [P, 2, NT, NH, VW])
        xn = sb("xn", [P, NT, DIM])
        ht = sb("ht", [P, 2, SEQ])
        part_h = sb("part_h", [P, 2, 2 * SEQ], BF16)
        part_m = sb("part_m", [P, 2, 2 * SEQ], BF16)
        part_l = sb("part_l", [P, 2, 2 * SEQ], BF16)
        rest = sb("rest", [P, 2, 2 * SEQ])
        mx = sb("mx", [P, 2, NT, 2, HU])
        mrest = sb("mrest", [P, NT * 2, HU])
        nm = sb("nm", [P, 2, NT * 2, 3, HU], BF16)
        nmt = sb("nmt", [MAX_ROWS * HU, 2, SEQ], BF16)
        ot = sb("ot", [P, 2, 4, SEQ])
        rec = sb("rec", [P, 2 * HU])
        on2 = sb("on2", [P, NT, NH, 2, 2 * DH])
        o = sb("o", [P, NT * NH, 2 * DH])
        on_tok = sb("on_tok", [P, NT, NH * 2 * DH])
        rms_ss = sb("rms_ss", [P, NT * NH])
        osq = sb("osq", [P, NT * NH, 2 * DH])
        ont = sb("ont", [P, 2, SEQ])
        stats = sb("stats", [P, 2, NT, 6])
        mvs = sb("mvs", [P, 2, NT, 2])
        neg_mr = sb("neg_mr", [P, 2 * NT])
        NV = NT * NH + 2 * NT
        var = sb("var", [P, NV])
        rstd = sb("rstd", [P, NV])
        nt1 = sb("nt1", [P, NV])
        nt2 = sb("nt2", [P, NV])
        mods = sb("mods", [P, 2, 3, DIM])
        xtmp = sb("xtmp", [P, NT, DIM])
        h2 = sb("h2", [P, 2, 2, NT, RW])
        h2t = sb("h2t", [P, SEQ])
        lg = sb("lg", [P, NT, NE])
        top8 = sb("top8", [P, NT, 8])
        top8i = sb("top8i", [P, NT, 8], U32)
        topf = sb("topf", [P, 2, NT])
        chosen = sb("chosen", [P, 2 * NT, NE])
        both = sb("both", [P, NT, NE], BF16)
        gdiff = sb("gdiff", [P, NT])
        gexp = sb("gexp", [P, NT])
        gden = sb("gden", [P, NT])
        carry = sb("carry", [P, NE])
        pos = sb("pos", [P, NT, NE])
        posm = sb("posm", [P, 2 * NT, NE])
        posf = sb("posf", [P, 2 * NT])
        idx = sb("idx", [P, 2, 2 * NT], I32)
        pairno = sb("pairno", [P, 2 * NT])
        posm_ramp = sb("posm_ramp", [P, NE])
        ends = sb("ends", [P, NE])
        endi = sb("endi", [P, NE], I32)
        ntil = sb("ntil", [P, NE])
        first = sb("first", [P, NE])
        jump = sb("jump", [P, NE])
        tileno = sb("tileno", [P, FFN_TILES])
        fill = sb("fill", [P, RW])
        rows_hi = sb("rows_hi", [P, 2, P], F32R)
        rows_lo = sb("rows_lo", [P, 2, P], F32R)
        tile_row = sb("tile_row", [P, FFN_TILES], I32)
        tile_exp = sb("tile_exp", [P, FFN_TILES], I32)

        maskf = ont[:, 0, 0:P]
        beforef = ont[:, 1, 0:P]
        lamv = rest[:, 0, :].rearrange("p (j k) -> p j k", j=4)
        mtmp = rest[0:NB, 1, 0:2 * DIM].rearrange("p (j k) -> p j k", j=2)
        w_mod_sb = probs[:, 0, 0:2, :].rearrange("p a k -> p (a k)")[:, 0:6 * DIM]

        p_exp = ps("p_exp", [P, 3, BANK])
        p_max = ps("p_max", [P, 2, 2 * SEQ])
        p_out = ps("p_out", [P, 2, SEQ])
        p_mix = ps("p_mix", [P, 2, 2 * SEQ])

        cond_loaded = sem("cond_loaded")
        consts_loaded = sem("consts_loaded")
        setup_g = sem("setup_g")
        waits_met = sem("waits_met")
        ffn_w_loaded = sem("ffn_w_loaded")
        setup_v = sem("setup_v")
        setup_a = sem("setup_a")
        setup_t = sem("setup_t")
        mods_saved = sem("mods_saved")
        x_loaded = [ev(f"x_loaded{i}", 16) for i in range(2)]
        mods_loaded = [ev(f"mods_loaded{i}", 16) for i in range(2)]
        stats1 = ev("stats1", NT + NT)
        xn_ready = ev("xn_ready", NT)
        xt_ps = ev("xt_ps")
        ht_ready = ev("ht_ready")
        proj_ps = ev("proj_ps", 2)
        h_ready = ev("h_ready", 2)
        r_ready = ev("r_ready", 2)
        m_ready = ev("m_ready", 2)
        l_ready = ev("l_ready", 2)
        NSAVE = SLOTS + 3
        parts_saved = ev("parts_saved", 16 * NSAVE)
        NLOAD = 1 + 2 * len(K_RUNS)
        unit_loaded = [ev(f"unit_loaded{w}", 16 * NLOAD) for w in range(2)]
        v_ps = ev("v_ps")
        v_ready = ev("v_ready")
        max_ps = ev("max_ps", NBANKS)
        max_done = ev("max_done", NBANKS)
        nm_step = ev("nm_step", 2 * 4)
        nm_ps = ev("nm_ps", 2)
        nmt_ready = ev("nmt_ready", 2)
        nm_saved = ev("nm_saved", 32)
        nm_loaded = [ev(f"nm_loaded{w}", 16) for w in range(2)]
        exp_ps = ev("exp_ps", NBANKS)
        exp_done = ev("exp_done", NBANKS)
        masked = ev("masked", NBANKS)
        pv_done = ev("pv_done", PAIRS)
        ot_ready = ev("ot_ready", PAIRS // 2)
        ot_ps = ev("ot_ps", 4)
        rec_step = ev("rec_step", 8)
        on2_ready = ev("on2_ready", 4)
        o_ready = ev("o_ready")
        osq_ready = ev("osq_ready")
        rms_sum = ev("rms_sum")
        newton = sem("newton")
        on_ready = ev("on_ready")
        ont_ps = ev("ont_ps")
        ont_ready = ev("ont_ready")
        wo_ps = ev("wo_ps")
        attn_scaled = ev("attn_scaled")
        x1_ready = ev("x1_ready")
        stats2 = ev("stats2", NT + NT)
        xn2_ready = ev("xn2_ready", NT)
        h2_step = ev("h2_step", 2)
        h2_copied = ev("h2_copied")
        h2t_ps = ev("h2t_ps")
        h2t_ready = ev("h2t_ready")
        lg_ps = ev("lg_ps")
        route = ev("route", ROUTE_STEPS)
        gexp_ready = ev("gexp_ready")
        rank_ps = ev("rank_ps")
        scattered = [ev(f"scattered{i}", 64) for i in range(2)]

        w_split = sem("w_split")
        tables = sem("tables")
        filled = sem("filled")
        rows_loaded = [sem(f"rows_loaded{r}") for r in range(RING)]
        row_t_ps = sem("row_t_ps")
        row_hi_ready = sem("row_hi_ready")
        row_t_ready = sem("row_t_ready")
        gate_ps = sem("gate_ps")
        up_ps = sem("up_ps")
        gate_done = sem("gate_done")
        hid_ready = sem("hid_ready")
        hid_t_ps = sem("hid_t_ps")
        hid_t_ready = sem("hid_t_ready")
        down_ps = sem("down_ps")
        rows_ready = sem("rows_ready")
        pairs_stored = [sem(f"pairs_stored{r}") for r in range(RING)]
        fin_loaded = [sem(f"fin_loaded{r}") for r in range(FIN_RING)]
        fin_step = sem("fin_step")
        fin_done = sem("fin_done")
        fin_stored = [sem(f"fin_stored{r}") for r in range(FIN_RING)]

        block = ctx.enter_context(nc.Block())

        CONSTS = 19
        LEAD, TAIL = 4, 3
        FIRST_FULL, LAST_FULL = TAIL + 1, NB - 1 - LEAD
        LOOPED = (LAST_FULL - FIRST_FULL + 1) // 2 * 2

        def iterations(eng, body):
            for i in range(-LEAD, FIRST_FULL):
                body(Batch(None, i))
            base = FIRST_FULL
            with eng.Fori(0, LOOPED // 2) as pair:
                body(Batch(pair, base))
                body(Batch(pair, base + 1))
            for i in range(base + LOOPED, NB + TAIL):
                body(Batch(None, i))

        def settle(eng):
            eng.sem_inc(waits_met, 1)

        def active(b):
            return not b.static or 0 <= b.c < NB

        MISC0 = [(ht_ready, 1, 2), (r_ready, 1, 2), (r_ready, 2, 2), (on2_ready, 4, -1),
                 (v_ready, 1, 1), (on2_ready, 1, 0)]
        MISC1 = [(ont_ready, 1, -2), (attn_scaled, 1, -2), (nmt_ready, 2, 0), (on2_ready, 3, -1),
                 (h2t_ready, 1, -3), (route, 1, -3), (nmt_ready, 1, 1), (route, ROUTE_CARRY, -3),
                 (on2_ready, 2, 0)]

        def mix_free(pe, i, bank, turn):
            readers = (MISC0, MISC1)[bank]
            for back in range(1, 4 * len(readers)):
                event, k, d = readers[(turn - back) % len(readers)]
                b = i.plus(d + (turn - back) // len(readers))
                if active(b):
                    wait(pe, event, b, k)
                    return
                if b.static and b.c < 0 and back > 3 * len(readers):
                    return


        lo_weights = kt[:].rearrange("p a t h k -> p (a t h k)").bitcast(F32)
        wg_lo, wu_lo = lo_weights[:, 0:NE * FF], lo_weights[:, NE * FF:2 * NE * FF]
        v_view = v[:].rearrange("p a t h k -> p (a t h k)")
        rows_in = v_view[:, 0:RING * RW].rearrange("p (r k) -> p r k", r=RING)
        act_g, hid = (ot[:, j, :, :].rearrange("p (a g) k -> p a (g k)", a=2) for j in range(2))
        hid_t = rest
        rows_out = on2[:].rearrange("p t h j d -> p (t h j d)").rearrange("p (r k) -> p r k", r=RING)
        table_view = qt[:].rearrange("p a h k -> p (a h k)").bitcast(F32)

        def split_weights(dve, c):
            V = nc.vector
            for w, lo in ((wg, wg_lo), (wu, wu_lo)):
                at = slice(c * FF, (c + 1) * FF)
                V.tensor_copy(lo[:, at].bitcast(F32R), w[:, at]).then_inc(w_split, 1)
                split_steps[0] += 1
                dve.wait_ge(w_split, split_steps[0])
                V.tensor_tensor(lo[:, at].bitcast(F32R), w[:, at], lo[:, at], ALU.subtract).then_inc(w_split, 1)
                split_steps[0] += 1
                dve.wait_ge(w_split, split_steps[0])
                V.tensor_copy(w[:, at].bitcast(F32R), w[:, at]).then_inc(w_split, 1)
                split_steps[0] += 1

        split_steps = [0]
        SPLIT_STEPS = 2 * 3 * NE
        p_gate = p_exp[:, 0:2, :]
        p_up = p_max
        p_hid_t = p_mix
        p_row_t = p_out[:, 0, 0:P]
        p_down = p_exp[:, 2, 0:DIM]
        pair_view = probs[:].rearrange("p a b k -> p (a b k)")
        NF = GROUP * NT * DIM
        fin_in = (qt[:].rearrange("p a h k -> p (a h k)").bitcast(F32)[:, 0:FIN_RING * 2 * NF]
                  .rearrange("p (a j c) -> p a j c", a=FIN_RING, j=2))
        fin_out = pair_view[:, 0:FIN_RING * NF].rearrange("p (a c) -> p a c", a=FIN_RING)
        fin_gb = (pair_view[:, FIN_RING * NF:FIN_RING * (NF + GROUP * DIM)]
                  .rearrange("p (a b c) -> p a b c", a=FIN_RING, b=GROUP))

        class Tile:

            def __init__(self, reg, c, ring=RING):
                self.static = reg is None
                self.reg, self.c, self.ring = reg, c, ring
                self.n = c if reg is None else reg * ring + c
                self.slot = c % ring
                self.turn = c // ring if reg is None else reg + c // ring

            def plus(self, d):
                return Tile(self.reg, self.c + d, self.ring)

        def t_active(j):
            return not j.static or 0 <= j.c < FFN_TILES

        def t_wait(eng, s, j, per=1, k=None):
            v = j.n * per + (per if k is None else k)
            if j.static and (j.c < 0 or v <= 0):
                return
            eng.wait_ge(s, v)

        def tiles(eng, body):
            for c in range(-1, RING):
                body(Tile(None, c))
            with eng.Fori(1, FFN_TILES // RING - 1) as reg:
                for c in range(RING):
                    body(Tile(reg, c))
            for c in range(FFN_TILES - RING, FFN_TILES + 2):
                body(Tile(None, c))

        def groups(eng, body):
            for c in range(FIN_RING):
                body(Tile(None, c, FIN_RING))
            with eng.Fori(1, NB // GROUP // FIN_RING) as reg:
                for c in range(FIN_RING):
                    body(Tile(reg, c, FIN_RING))

        TABLE_STEPS = 17

        def ffn_sp(sp):
            sp.wait_ge(tables, 1)
            for e in range(NE):
                start = sp.value_load(endi[0:1, e:e + 1], min_val=0, max_val=SORTED_ROWS - LAST_PADS * P)
                if e < NE - 1:
                    sp.dma_start(rows_sorted[bass.ds(start, P), :], fill[:, :]).then_inc(filled, 16)
                else:
                    sp.dma_start(rows_sorted[bass.ds(start, LAST_PADS * P), :].rearrange("(m p) r -> p m r", p=P),
                                 fill[:].unsqueeze(1).to_broadcast([P, LAST_PADS, RW])).then_inc(filled, 16)
            sp.wait_ge(tables, TABLE_STEPS)
            sp.wait_ge(filled, 16 * NE)
            for i in range(2):
                sp.wait_ge(scattered[i].sem, scattered[i].per * NB // 2)
            sp.wait_ge(pv_done.sem, PAIRS * NB)

            def load(j):
                if not t_active(j):
                    return
                if not (j.static and j.c < RING):
                    sp.wait_ge(pairs_stored[j.slot], 16 * j.turn)
                row = sp.value_load(tile_row[0:1, bass.ds(j.n, 1)], min_val=0, max_val=SORTED_ROWS - P)
                sp.dma_start(rows_in[:, j.slot, :], rows_sorted[bass.ds(row, P), :]).then_inc(rows_loaded[j.slot], 16)

            for c in range(RING):
                load(Tile(None, c))
            with sp.Fori(1, FFN_TILES // RING) as reg:
                for c in range(RING):
                    load(Tile(reg, c))
            for r in range(RING):
                sp.wait_ge(pairs_stored[r], 16 * (FFN_TILES // RING))

            def final(g):
                if not g.static:
                    sp.wait_ge(fin_done, (g.n - FIN_RING) + 1)
                for j in range(2):
                    sp.dma_start(fin_in[:, g.slot, j, :].rearrange("p (t c) -> p t c", c=DIM),
                                 pair_out[bass.ds(g.n * GROUP * SEQ + j * NB * SEQ, GROUP * SEQ), :]
                                 .rearrange("(t p) c -> p t c", p=P)).then_inc(fin_loaded[g.slot], 16)
                sp.dma_start(fin_gb[:, g.slot, :, :],
                             mod_rows[bass.ds(g.n * GROUP, GROUP), 3 * DIM:4 * DIM].unsqueeze(0)
                             .to_broadcast([P, GROUP, DIM])).then_inc(fin_loaded[g.slot], 16)

            groups(sp, final)

        def ffn_products(pe):
            pe.wait_ge(ffn_w_loaded, 48)
            pe.wait_ge(w_split, SPLIT_STEPS)
            pe.wait_ge(tables, TABLE_STEPS)

            def three_passes(to, par, hi, lo, w0):
                for k, (rows, w) in enumerate(((rows_hi, hi), (rows_hi, lo), (rows_lo, hi))):
                    m = nc.tensor.matmul(to, rows[:, par, :], w[:, bass.ds(w0, FF)].bitcast(F32R),
                                         start=(k == 0), stop=(k == 2))
                return m

            def body(j):
                j1, jt, jd = j.plus(1), j.plus(-1), j.plus(-2)
                if t_active(j):
                    w0 = pe.value_load(tile_exp[0:1, bass.ds(j.n, 1)], min_val=0, max_val=(NE - 1) * FF)
                if t_active(j1):
                    pe.wait_ge(rows_loaded[j1.slot], 16 * (j1.turn + 1))
                    t_wait(pe, row_t_ready, j1.plus(-1))
                    nc.tensor.transpose(p_row_t, rows_in[:, j1.slot, 0:DIM], idf[:]).then_inc(row_t_ps, 1)
                if t_active(j):
                    t_wait(pe, row_t_ready, j)
                    t_wait(pe, gate_done, j.plus(-2))
                    three_passes(p_gate[:, j.c % 2, :], j.c % 2, wg, wg_lo, w0).then_inc(gate_ps, 1)
                    t_wait(pe, hid_ready, j.plus(-2))
                    three_passes(p_up[:, j.c % 2, :], j.c % 2, wu, wu_lo, w0).then_inc(up_ps, 1)
                if t_active(jt):
                    t_wait(pe, hid_ready, jt)
                    t_wait(pe, hid_t_ready, jt.plus(-2))
                    for f in range(FCH):
                        m = nc.tensor.transpose(p_hid_t[:, jt.c % 2, f * P:(f + 1) * P], hid[:, jt.c % 2, f * P:(f + 1) * P], idf[:])
                    m.then_inc(hid_t_ps, 1)
                if t_active(jd):
                    w0 = pe.value_load(tile_exp[0:1, bass.ds(jd.n, 1)], min_val=0, max_val=(NE - 1) * FF)
                    t_wait(pe, hid_t_ready, jd)
                    t_wait(pe, rows_ready, jd.plus(-1))
                    for f in range(FCH):
                        m = nc.tensor.matmul(p_down, hid_t[:, jd.c % 2, f * P:(f + 1) * P],
                                             wd[:, bass.ds(w0 + f * P, P)], start=(f == 0), stop=(f == FCH - 1))
                    m.then_inc(down_ps, 1)

            tiles(pe, body)

        def ffn_activations(act):
            def body(j):
                jd = j.plus(-2)
                if t_active(j):
                    t_wait(act, gate_ps, j)
                    t_wait(act, hid_ready, j.plus(-2))
                    nc.scalar.activation(act_g[:, j.c % 2, :], p_gate[:, j.c % 2, :], ACT.Silu).then_inc(gate_done, 1)
                if t_active(jd):
                    t_wait(act, down_ps, jd)
                    if not (jd.static and jd.c < RING):
                        act.wait_ge(pairs_stored[jd.slot], 16 * jd.turn)
                    nc.scalar.activation(rows_out[:, jd.slot, :], p_down, ACT.Copy,
                                         scale=rows_in[:, jd.slot, DIM + 1:DIM + 2]).then_inc(rows_ready, 1)

            tiles(act, body)

            def final(g):
                act.wait_ge(fin_done, g.n + 1)
                act.dma_start(out[bass.ds(g.n * GROUP, GROUP)].rearrange("a (t p) c -> p (a t) c", p=P),
                              fin_out[:, g.slot, :].rearrange("p (t c) -> p t c", c=DIM)).then_inc(fin_stored[g.slot], 16)

            groups(act, final)
            for r in range(FIN_RING):
                act.wait_ge(fin_stored[r], 16 * (NB // GROUP // FIN_RING))

        def ffn_vector(dve):
            V = nc.vector
            count = [0]

            def step(ins):
                count[0] += 1
                ins.then_inc(tables, 1)
                dve.wait_ge(tables, count[0])

            dve.wait_ge(route.sem, ROUTE_STEPS * NB)
            step(V.tensor_copy(endi[:], carry[:]))
            step(V.tensor_tensor(ends[:], carry[:], posm_ramp[:], ALU.subtract))
            step(V.tensor_scalar(ntil[:].bitcast(I32), ends[:], float(P - 1), None, ALU.add))
            step(V.tensor_scalar(ntil[:].bitcast(I32), ntil[:].bitcast(I32), P.bit_length() - 1, None, ALU.logical_shift_right))
            step(V.tensor_copy(first[:], ntil[:].bitcast(I32)))
            step(V.tensor_scalar(jump[:], first[:], -float(P), float(REGION), ALU.mult, ALU.add))
            for e in range(1, NE - 1):
                step(V.tensor_tensor(first[:, e:e + 1], first[:, e:e + 1], first[:, e - 1:e], ALU.add))
            ge = table_view[:, 0:FFN_TILES * (NE - 1)].rearrange("p (j e) -> p j e", e=NE - 1)
            sums = table_view[:, FFN_TILES * NE:FFN_TILES * (NE + 1)]
            dve.wait_ge(pv_done.sem, PAIRS * NB)
            step(V.tensor_tensor(ge, tileno[:].unsqueeze(2).to_broadcast([P, FFN_TILES, NE - 1]),
                                 first[:, 0:NE - 1].unsqueeze(1).to_broadcast([P, FFN_TILES, NE - 1]), ALU.is_ge))
            step(V.reduce_sum(sums, ge, AX.X))
            V.tensor_scalar(tile_exp[:], sums, float(FF), None, ALU.mult)
            step(V.tensor_tensor(ge, ge, jump[:, 0:NE - 1].unsqueeze(1).to_broadcast([P, FFN_TILES, NE - 1]), ALU.mult))
            step(V.reduce_sum(sums, ge, AX.X))
            step(V.scalar_tensor_tensor(tile_row[:], tileno[:], float(P), sums, ALU.mult, ALU.add))
            assert count[0] == TABLE_STEPS, count
            for c in range(2 * TAIL, NE):
                split_weights(dve, c)
            assert split_steps[0] == SPLIT_STEPS

            def body(j):
                j1, jt = j.plus(1), j.plus(-1)
                if t_active(j1):
                    t_wait(dve, row_t_ps, j1)
                    t_wait(dve, up_ps, j1.plus(-2))
                    V.tensor_copy(rows_hi[:, j1.c % 2, :], p_row_t).then_inc(row_hi_ready, 1)
                    t_wait(dve, row_hi_ready, j1)
                    V.tensor_tensor(rows_lo[:, j1.c % 2, :], p_row_t, rows_hi[:, j1.c % 2, :].bitcast(F32), ALU.subtract).then_inc(row_t_ready, 1)
                if t_active(j):
                    t_wait(dve, gate_done, j)
                    t_wait(dve, up_ps, j)
                    t_wait(dve, hid_t_ps, j.plus(-2))
                    V.tensor_tensor(hid[:, j.c % 2, :], act_g[:, j.c % 2, :], p_up[:, j.c % 2, :], ALU.mult).then_inc(hid_ready, 1)
                if t_active(jt):
                    t_wait(dve, hid_t_ps, jt)
                    t_wait(dve, down_ps, jt.plus(-2))
                    V.tensor_copy(hid_t[:, jt.c % 2, :], p_hid_t[:, jt.c % 2, :]).then_inc(hid_t_ready, 1)

            tiles(dve, body)

            def final(g):
                dve.wait_ge(fin_loaded[g.slot], 48 * (g.turn + 1))
                if not g.static:
                    dve.wait_ge(fin_stored[g.slot], 16 * g.turn)
                V.tensor_tensor(fin_out[:, g.slot, :], fin_in[:, g.slot, 0, :], fin_in[:, g.slot, 1, :], ALU.add).then_inc(fin_step, 1)
                dve.wait_ge(fin_step, 2 * g.n + 1)
                fo = fin_out[:, g.slot, :].rearrange("p (b t c) -> p b t c", b=GROUP, c=DIM)
                V.tensor_tensor(fo, fo, fin_gb[:, g.slot, :, :].unsqueeze(2).to_broadcast([P, GROUP, NT, DIM]), ALU.mult).then_inc(fin_step, 1)

            groups(dve, final)

        def ffn_pool(pool):
            def store(j):
                t_wait(pool, rows_ready, j)
                settle(pool)
                nc.gpsimd.indirect_dma_start(pair_out, bass.IndirectOffsetOnAxis(rows_in[:, j.slot, DIM:DIM + 1].bitcast(U32), 0),
                                             rows_out[:, j.slot, :], None, bounds_check=ROUTED - 1, oob_is_err=False
                                             ).then_inc(pairs_stored[j.slot], 16)

            for c in range(RING):
                store(Tile(None, c))
            with pool.Fori(1, FFN_TILES // RING) as reg:
                for c in range(RING):
                    store(Tile(reg, c))

            def final(g):
                pool.wait_ge(fin_step, 2 * g.n + 2)
                nc.gpsimd.tensor_tensor(fin_out[:, g.slot, :], fin_out[:, g.slot, :],
                                        xres[:, bass.ds(g.n * GROUP * SEQ, GROUP * SEQ)], ALU.add).then_inc(fin_done, 1)

            groups(pool, final)

        @block.sync
        def _(sp):
            for dst, src in ((ct[:], c_t), (w_mod_sb, w_mod)):
                sp.dma_start(dst, src).then_inc(cond_loaded, 16)
            for j in range(4):
                sp.dma_start(lamv[:, j, :], lambdas[j]).then_inc(consts_loaded, 16)
            for dst, src in ((idf[:], ident), (maskf, mask_q), (beforef, before), (iota8[:], iota),
                             (wqk[:], w_qk), (wv[:], w_v), (wo[:], w_o), (rmsc[:], rms_col), (rw[:], router_w),
                             (rb[:], router_b), (posm_ramp[:], ramp), (pairno[:], pair_no), (tileno[:], tile_no),
                             (fill[:], filler)):
                sp.dma_start(dst, src).then_inc(consts_loaded, 16)
            sp.dma_start(kt[QK_ROWS:ALL_ROWS, :, :, :, :].rearrange("p a t h k -> p a t (h k)").bitcast(I32),
                         max_ones).then_inc(consts_loaded, 16)

            def body(i):
                b = i.plus(4)
                if active(b):
                    wait(sp, stats1, b.plus(-2), 1)
                    sp.dma_start(xres[:, bass.ds(b.n * SEQ, SEQ)].rearrange("p (t c) -> p t c", t=NT),
                                 x[bass.ds(b.n, 1)].rearrange("a (t p) c -> p (a t) c", p=P)
                                 ).then_inc(x_loaded[b.par].sem, 16)
                if i.static and i.c == 1 - LEAD:
                    sp.wait_ge(setup_v, SETUP_ROWS)
                    sp.dma_start(mod_rows.rearrange("b (j c) -> b j c", j=4), mrow[:, :, :]).then_inc(mods_saved, 16)
                b = i.plus(1)
                if active(b):
                    load_unit(b, 1)
                b = i
                if active(b):
                    move_max(b, 1)
                b = i.plus(2)
                if active(b):
                    wait(sp, l_ready, b)
                    for s, part in enumerate(Q_SLOTS):
                        buf = (part_h, part_m, part_l)[part]
                        sp.dma_start(q_parts[bass.ds(b.n, 1), :, s, :, :, :].rearrange("a t d h k -> (a d h) t k"),
                                     buf[:, 0, :].rearrange("p (t k) -> p t k", t=2)
                                     ).then_inc(parts_saved.sem, 16)
                    for part, buf in enumerate((part_h, part_m, part_l)):
                        sp.dma_start(k_parts[bass.ds(b.n, 1), :, part, :, :, :].rearrange("a t d h k -> (a d h) t k"),
                                     buf[:, 1, :].rearrange("p (t k) -> p t k", t=2)
                                     ).then_inc(parts_saved.sem, 16)
                    wait(sp, parts_saved, b)
                    load_unit(b, 0)
                b = i.plus(1)
                if active(b):
                    move_max(b, 0)
                b = i.plus(-1)
                if active(b):
                    if b.static and b.c == 0:
                        sp.wait_ge(mods_saved, 16)
                    wait(sp, h2_step, b.plus(-2))
                    sp.dma_start(mods[:, b.par, :, :],
                                 mod_rows[bass.ds(b.n, 1), 0:3 * DIM].rearrange("a (j c) -> a j c", j=3)
                                 .to_broadcast([P, 3, DIM])).then_inc(mods_loaded[b.par].sem, 16)

            def load_unit(b, w):
                slot = 2 * b.par + w
                wait(sp, exp_ps, b.plus(-2), NBANKS // 2 * (w + 1))
                wait(sp, parts_saved, b)
                sp.dma_start(qt[0:QK_ROWS, slot, :, :],
                             q_parts[bass.ds(b.n, 1), :, :, :, w * HU:(w + 1) * HU, :]
                             .rearrange("a t s d h k -> (a t s d) h k")).then_inc(unit_loaded[w].sem, 16)
                for t in range(2):
                    for s0, ns in K_RUNS:
                        r0 = t * HALF_ROWS + s0 * DH
                        sp.dma_start(kt[r0:r0 + ns * DH, slot, t, :, :],
                                     k_parts[bass.ds(b.n, 1), t, 0:ns, :, w * HU:(w + 1) * HU, :]
                                     .rearrange("a s d h k -> (a s d) h k")).then_inc(unit_loaded[w].sem, 16)

            def move_max(b, w):
                wait(sp, nmt_ready, b, w + 1)
                sp.dma_start(max_parts[bass.ds(b.n, 1), w].rearrange("a r h k -> (a r h) k"),
                             nmt[:, w, :]).then_inc(nm_saved.sem, 16)
                wait(sp, nm_saved, b, 16 * (w + 1))
                sp.dma_start(qt[QK_ROWS:ALL_ROWS, 2 * b.par + w, :, :],
                             max_parts[bass.ds(b.n, 1), w].rearrange("a r h k -> (a r) h k")
                             ).then_inc(nm_loaded[w].sem, 16)

            iterations(sp, body)
            ffn_sp(sp)

        @block.tensor
        def _(pe):
            pe.wait_ge(setup_v, SETUP_SILU)
            for j in range(2):
                m = nc.tensor.matmul(p_mix[:, 0, j * NB:(j + 1) * NB], w_mod_sb[:, j * DIM:(j + 1) * DIM],
                                     silu_t[:, 2, :], start=True, stop=True)
            nc.tensor.matmul(p_max[0:NB, 0, 0:2 * DIM], silu_t[:, 2, :], w_mod_sb[:, 2 * DIM:4 * DIM], start=True, stop=True)
            m = nc.tensor.matmul(p_max[0:NB, 1, 0:2 * DIM], silu_t[:, 2, :], w_mod_sb[:, 4 * DIM:6 * DIM], start=True, stop=True)
            m.then_inc(setup_t, 1)
            pe.wait_ge(setup_v, SETUP_DONE)
            pe.wait_ge(setup_a, 2)

            def scores_for_max(b, h, n, rows):
                w, h8, bank = h // HU, h % HU, n % 2
                slot = 2 * b.par + w
                if n in (0, NBANKS // 2):
                    wait(pe, unit_loaded[w], b)
                if n >= 2:
                    wait(pe, max_done, b, n - 1)
                else:
                    wait(pe, max_done, b.plus(-1), NBANKS - 1 + n)
                if rows == 1:
                    for t in range(2):
                        nc.tensor.matmul(p_max[:, bank, t * SEQ:(t + 1) * SEQ], qt[0:QK_ROWS, slot, h8, P:SEQ],
                                         kt[0:QK_ROWS, slot, t, h8, :], start=(t == 0), stop=False)
                    m = nc.tensor.matmul(p_max[:, bank, :].rearrange("p (t k) -> p t k", t=2)[:, :, P:SEQ], idb[:],
                                         mask4[:, 0:2, :], start=False, stop=True)
                else:
                    for hh in range(2):
                        for t in range(2):
                            c = (2 * t + hh) * P
                            nc.tensor.matmul(p_max[:, bank, c:c + P], qt[0:QK_ROWS, slot, h8 - 1 + hh, 0:P],
                                             kt[0:QK_ROWS, slot, t, h8 - 1 + hh, 0:P],
                                             start=(t == 0 and hh == 0), stop=False)
                    m = nc.tensor.matmul(p_max[:, bank, :].rearrange("p (j k) -> p j k", j=4), idb[:], mask4[:],
                                         start=False, stop=True)
                m.then_inc(max_ps.sem, 1)

            def scores_for_exp(b, h, n, tile):
                w, h8, bank = h // HU, h % HU, n % 3
                slot = 2 * b.par + w
                if n in (0, NBANKS // 2):
                    wait(pe, nm_loaded[w], b)
                if n >= 3:
                    wait(pe, exp_done, b, n - 2)
                else:
                    wait(pe, exp_done, b.plus(-1), NBANKS - 2 + n)
                if tile == 0:
                    for t in range(2):
                        m = nc.tensor.matmul(p_exp[:, bank, t * SEQ:(t + 1) * SEQ], kt[0:ALL_ROWS, slot, t, h8, 0:P],
                                             qt[0:ALL_ROWS, slot, h8, :], start=True, stop=True)
                else:
                    for hh in range(2):
                        for t in range(2):
                            c = (2 * hh + t) * P
                            m = nc.tensor.matmul(p_exp[:, bank, c:c + P], kt[0:ALL_ROWS, slot, t, h8 - 1 + hh, P:SEQ],
                                                 qt[0:ALL_ROWS, slot, h8 - 1 + hh, P:SEQ], start=True, stop=True)
                m.then_inc(exp_ps.sem, 1)

            def outputs(b, g):
                if g == 0:
                    wait(pe, v_ready, b)
                wait(pe, masked, b, 3 * (g + 1))
                if g % 2 == 0:
                    wait(pe, ot_ready, b, g // 2) if g else wait(pe, ot_ready, b.plus(-1))
                for tile in range(NT):
                    n = SEQ if tile == 0 else P
                    for j in range(4):
                        src = (probs[:, g % 2, j // 2, (j % 2) * SEQ:(j % 2 + 1) * SEQ] if tile == 0
                               else probs[:, g % 2, 2, j * P:(j + 1) * P])
                        m = nc.tensor.matmul(p_out[32 * j:32 * j + 32, g % 2, SEQ - n:SEQ],
                                             v[:, b.par, tile, 2 * g + j // 2, :], src,
                                             start=(tile == 0), stop=(tile == 1))
                m.then_inc(pv_done.sem, 1)

            def outputs_to_rows(i, b, w, tile, bank, turn):
                mix_free(pe, i, bank, turn)
                wait(pe, ot_ready, b, 2 * (w + 1))
                for g in range(4):
                    m = nc.tensor.transpose(p_mix[:, bank, g * P:(g + 1) * P], ot[:, w, g, tile * P:(tile + 1) * P], idf[:])
                m.then_inc(ot_ps.sem, 1)

            def project(i, b, j, turn):
                mix_free(pe, i, 0, turn)
                for t in range(2):
                    m = nc.tensor.matmul(p_mix[:, 0, t * SEQ:(t + 1) * SEQ], wqk[:, 2 * j + t, :], ht[:, b.par, :],
                                         start=True, stop=True)
                m.then_inc(proj_ps.sem, 1)

            def max_to_rows(i, b, w, turn):
                mix_free(pe, i, 1, turn)
                wait(pe, nm_step, b, 4 * (w + 1))
                settle(pe)
                pm = p_mix[:, 1, 0:P].bitcast(BF16)
                for tile in range(NT):
                    m = nc.tensor.transpose(pm[0:MAX_ROWS * HU, tile * P:(tile + 1) * P],
                                            nm[:, w, 2 * tile:2 * tile + 2, :, :].rearrange("p t s h -> p (t s h)"), idb[:])
                m.then_inc(nm_ps.sem, 1)

            def body(i):
                bA, bV, b1, b2, bC, bW, bR = (i.plus(d) for d in (2, 1, 1, 0, -1, -2, -3))
                for s in range(NH):
                    n = s + s // 2
                    if active(b1):
                        scores_for_max(b1, s, n, 1)
                    if active(b2):
                        scores_for_exp(b2, s, n, 0)
                    if active(b1) and s % 2:
                        scores_for_max(b1, s, n + 1, 0)
                    if active(b2) and s % 2:
                        scores_for_exp(b2, s, n + 1, 1)
                    if s % 2:
                        g = s // 2 - 1
                        if g >= 0 and active(b2):
                            outputs(b2, g)
                        if g < 0 and active(bC):
                            outputs(bC, g + PAIRS)
                    if s == 0 and active(bA):
                        mix_free(pe, i, 0, 0)
                        wait(pe, xn_ready, bA)
                        for tile in range(NT):
                            m = nc.tensor.transpose(p_mix[:, 0, tile * P:(tile + 1) * P], xn[:, tile, :], idf[:])
                        m.then_inc(xt_ps.sem, 1)
                    if s == 1 and active(bW):
                        mix_free(pe, i, 1, 0)
                        wait(pe, on_ready, bW)
                        for half in range(2):
                            for tile in range(NT):
                                m = nc.tensor.transpose(
                                    p_mix[:, 1, (2 * half + tile) * P:(2 * half + tile + 1) * P],
                                    on_tok[:, tile, half * P:(half + 1) * P], idf[:])
                        m.then_inc(ont_ps.sem, 1)
                    if s == 1 and active(bA):
                        wait(pe, ht_ready, bA)
                        project(i, bA, 0, 1)
                    if s == 2 and active(bW):
                        mix_free(pe, i, 1, 1)
                        wait(pe, ont_ready, bW)
                        for tile in range(NT):
                            for half in range(2):
                                m = nc.tensor.matmul(p_mix[:, 1, tile * P:(tile + 1) * P],
                                                     ont[:, half, tile * P:(tile + 1) * P], wo[:, half, :],
                                                     start=(half == 0), stop=(half == 1))
                        m.then_inc(wo_ps.sem, 1)
                    if s == 3 and active(b2):
                        max_to_rows(i, b2, 1, 2)
                    if s == 3 and active(bA):
                        project(i, bA, 1, 2)
                    if s == 4 and active(bC):
                        outputs_to_rows(i, bC, 1, 0, 1, 3)
                    if s == 5 and active(bC):
                        outputs_to_rows(i, bC, 1, 1, 0, 3)
                    if s == 6 and active(bR):
                        mix_free(pe, i, 1, 4)
                        wait(pe, h2_step, bR)
                        for tile in range(NT):
                            m = nc.tensor.transpose(p_mix[:, 1, tile * P:(tile + 1) * P], h2[:, bR.par, 0, tile, 0:DIM], idf[:])
                        m.then_inc(h2t_ps.sem, 1)
                    if s == 7 and active(bR):
                        mix_free(pe, i, 1, 5)
                        wait(pe, h2t_ready, bR)
                        for tile in range(NT):
                            m = nc.tensor.matmul(p_mix[:, 1, tile * NE:(tile + 1) * NE], h2t[:, tile * P:(tile + 1) * P],
                                                 rw[:], start=True, stop=True)
                        m.then_inc(lg_ps.sem, 1)
                    if s == 8 and active(bV):
                        mix_free(pe, i, 0, 4)
                        wait(pe, ht_ready, bV)
                        for tile in range(NT):
                            m = nc.tensor.matmul(p_mix[:, 0, tile * SEQ:(tile + 1) * SEQ],
                                                 ht[:, bV.par, tile * P:(tile + 1) * P], wv[:], start=True, stop=True)
                        m.then_inc(v_ps.sem, 1)
                    if s == 9 and active(b1):
                        max_to_rows(i, b1, 0, 6)
                    if s == 10 and active(bR):
                        mix_free(pe, i, 1, 7)
                        wait(pe, route, bR, ROUTE_BOTH)
                        nc.tensor.matmul(p_mix[:, 1, 0:2 * NE], beforeb[:], both[:].rearrange("p t e -> p (t e)"),
                                         start=True, stop=False)
                        nc.tensor.matmul(p_mix[:, 1, NE:2 * NE], onesb[:], both[:, 0, :], start=False, stop=True)
                        for tile in range(NT):
                            m = nc.tensor.matmul(p_mix[:, 1, 2 * NE:3 * NE], onesb[:], both[:, tile, :],
                                                 start=(tile == 0), stop=(tile == NT - 1))
                        m.then_inc(rank_ps.sem, 1)
                    if s == 11 and active(b2):
                        outputs_to_rows(i, b2, 0, 0, 0, 5)
                    if s == 14 and active(b2):
                        outputs_to_rows(i, b2, 0, 1, 1, 8)

            iterations(pe, body)
            ffn_products(pe)

        @block.scalar
        def _(act):
            act.wait_ge(cond_loaded, 32)
            nc.scalar.activation(silu_t[:, 0, :], ct[:], ACT.Exp, scale=-1.0).then_inc(setup_a, 1)
            act.wait_ge(setup_v, SETUP_LAM)
            nc.scalar.activation(lams[:], lams[:], ACT.Exp).then_inc(setup_a, 1)
            for dst, src in ((wg, gate_w), (wu, up_w), (wd, down_w)):
                act.dma_start(dst[:], src).then_inc(ffn_w_loaded, 16)
            act.wait_ge(setup_v, SETUP_DONE)
            act.wait_ge(setup_g, 2)

            def copy_outputs(b, q):
                wait(act, pv_done, b, 2 * (q + 1))
                wait(act, ot_ps, b.plus(-1), 2 * (q // 2 + 1))
                nc.scalar.copy(ot[:, q // 2, 2 * (q % 2):2 * (q % 2) + 2, :], p_out[:, :, :]).then_inc(ot_ready.sem, 1)

            def exp_bank(b, n):
                g, k = n // 3, n % 3
                wait(act, exp_ps, b, n + 1)
                if k == 0:
                    wait(act, pv_done, b, g - 1) if g >= 2 else wait(act, pv_done, b.plus(-1), PAIRS - 1 + g)
                nc.scalar.activation(probs[:, g % 2, k, :], p_exp[:, k, :], ACT.Exp, scale=SCALE).then_inc(exp_done.sem, 1)

            def copy_max(b, w):
                wait(act, nm_ps, b, w + 1)
                wait(act, nm_saved, b.plus(-1), 16 * (w + 1))
                pm = p_mix[:, 1, 0:P].bitcast(BF16)
                nc.scalar.copy(nmt[:, w, :], pm[0:MAX_ROWS * HU, :]).then_inc(nmt_ready.sem, 1)

            def high_part(b, j):
                wait(act, proj_ps, b, j + 1)
                wait(act, parts_saved, b.plus(-1))
                nc.scalar.copy(part_h[:, j, :], p_mix[:, 0, :]).then_inc(h_ready.sem, 1)

            def middle_part(b, j):
                wait(act, r_ready, b, j + 1)
                nc.scalar.copy(part_m[:, j, :], rest[:, j, :]).then_inc(m_ready.sem, 1)

            def body(i):
                bL, bA, bV, b1, b2, bC, bW, bR = (i.plus(d) for d in (3, 2, 1, 1, 0, -1, -2, -3))
                for s in range(NH):
                    if active(b2):
                        exp_bank(b2, s + s // 2)
                        if s % 2:
                            exp_bank(b2, s + s // 2 + 1)
                    if s == 0 and active(bA):
                        wait(act, xt_ps, bA)
                        wait(act, v_ps, bA.plus(-2))
                        nc.scalar.activation(ht[:, bA.par, :], p_mix[:, 0, 0:SEQ], ACT.Identity,
                                             bias=sa_t[:, bass.ds(bA.n, 1)], scale=ca_t[:, bass.ds(bA.n, 1)]
                                             ).then_inc(ht_ready.sem, 1)
                    if s == 1 and active(bW):
                        wait(act, ont_ps, bW)
                        nc.scalar.copy(ont[:].rearrange("p a k -> p (a k)"), p_mix[:, 1, :]).then_inc(ont_ready.sem, 1)
                    if s in (6, 10, 14) and active(b2):
                        copy_outputs(b2, (s - 6) // 4)
                    if s == 2 and active(bC):
                        copy_outputs(bC, 3)
                    if s == 1 and active(bA):
                        high_part(bA, 0)
                    if s == 3 and active(bA):
                        middle_part(bA, 0)
                    if s == 3 and active(b2):
                        copy_max(b2, 1)
                    if s == 3 and active(bA):
                        high_part(bA, 1)
                    if s == 5 and active(bA):
                        middle_part(bA, 1)
                    if s == 6 and active(bR):
                        wait(act, h2t_ps, bR)
                        nc.scalar.copy(h2t[:], p_mix[:, 1, 0:SEQ]).then_inc(h2t_ready.sem, 1)
                    if s == 7 and active(bR):
                        wait(act, h2_step, bR)
                        nc.scalar.copy(h2[:, bR.par, 1, :, 0:DIM], h2[:, bR.par, 0, :, 0:DIM]).then_inc(h2_copied.sem, 1)
                    if s == 8 and active(bV):
                        wait(act, v_ps, bV)
                        wait(act, pv_done, bV.plus(-2))
                        nc.scalar.copy(v[:, bV.par, :, :, 0:2 * DH].rearrange("p t h d -> p (t h) d"),
                                       p_mix[:, 0, :].rearrange("p (j d) -> p j d", d=2 * DH)).then_inc(v_ready.sem, 1)
                    if s == 9 and active(b1):
                        copy_max(b1, 0)
                    if s == 10 and active(bR):
                        wait(act, route, bR, ROUTE_DIFF)
                        nc.scalar.activation(gexp[:], gdiff[:], ACT.Exp).then_inc(gexp_ready.sem, 1)
                    if s == 15 and (active(bL) or active(bW)):
                        act.wait_ge(newton, NEWTON * (i.n + LEAD))
                    if s == 15 and active(bL):
                        wait(act, xt_ps, bL.plus(-1))
                        settle(act)
                        for tile in range(NT):
                            c = NT * NH + tile
                            nc.scalar.activation(xn[:, tile, :], xres[:, bass.ds(bL.n * SEQ + tile * DIM, DIM)], ACT.Identity,
                                                 bias=neg_mr[:, tile:tile + 1], scale=rstd[:, c:c + 1]).then_inc(xn_ready.sem, 1)
                    if s == 15 and active(bW):
                        if not (bW.static and bW.c < 2):
                            wait_half(act, scattered[bW.par], bW.plus(-2))
                        wait(act, h2t_ps, bW.plus(-2))
                        wait(act, h2_copied, bW.plus(-2))
                        settle(act)
                        for tile in range(NT):
                            c = NT * NH + NT + tile
                            nc.scalar.activation(h2[:, bW.par, 0, tile, 0:DIM], xres[:, bass.ds(bW.n * SEQ + tile * DIM, DIM)],
                                                 ACT.Identity, bias=neg_mr[:, NT + tile:NT + tile + 1],
                                                 scale=rstd[:, c:c + 1]).then_inc(xn2_ready.sem, 1)

            iterations(act, body)
            ffn_activations(act)

        @block.vector
        def _(dve):
            count = [0]

            def step(ins):
                count[0] += 1
                ins.then_inc(setup_v, 1)
                dve.wait_ge(setup_v, count[0])

            V = nc.vector
            V.memset(onesb[:], 1.0)
            V.memset(rstd[:], 1.0)
            V.memset(rms_ss[:], 1.0)
            V.memset(mvs[:], 1.0)
            V.memset(var[:], 1.0)
            dve.wait_ge(setup_a, 1)
            step(V.tensor_scalar(silu_t[:, 0, :], silu_t[:, 0, :], 1.0, None, ALU.add))
            step(V.reciprocal(silu_t[:, 1, :], silu_t[:, 0, :]))
            step(V.tensor_tensor(silu_t[:, 2, :], silu_t[:, 1, :], ct[:], ALU.mult))
            assert count[0] == SETUP_SILU
            dve.wait_ge(consts_loaded, 16 * CONSTS)
            for j in range(2):
                last = V.tensor_tensor(lamv[:, 2 * j, :], lamv[:, 2 * j, :], lamv[:, 2 * j + 1, :], ALU.mult)
            step(last)
            for j in range(2):
                last = V.reduce_sum(lams[:, j, :], lamv[:, 2 * j, :].rearrange("p (h d) -> p h d", d=DH), AX.X)
            step(last)
            assert count[0] == SETUP_LAM
            V.tensor_copy(idb[:], idf[:])
            V.tensor_copy(beforeb[:], beforef)
            for j in range(4):
                V.tensor_copy(mask4[:, j, :], maskf)
            V.tensor_copy(carry[:], posm_ramp[:])
            step(V.tensor_scalar(wo[:], wo[:], rmsc[:, 0:1], 1.0 - LAMBDA_INIT, ALU.mult, ALU.mult))
            dve.wait_ge(setup_t, 1)
            V.tensor_copy(sa_t[:], p_mix[:, 0, 0:NB])
            V.tensor_scalar(ca_t[:], p_mix[:, 0, NB:2 * NB], 1.0, None, ALU.add)
            V.tensor_scalar(mrow[:, 1, :], p_max[0:NB, 1, 0:DIM], 1.0, None, ALU.add)
            V.tensor_copy(mrow[:, 2, :], p_max[0:NB, 0, DIM:2 * DIM])
            for dst, src in ((0, p_max[0:NB, 0, 0:DIM]), (3, p_max[0:NB, 1, DIM:2 * DIM])):
                step(V.tensor_scalar(mtmp[:, 0, :], src, -1.0, 0.25, ALU.mult, ALU.max))
                step(V.tensor_tensor(mtmp[:, 0, :], mtmp[:, 0, :], src, ALU.max))
                step(V.tensor_scalar(mtmp[:, 1, :], src, 0.0, 2.0, ALU.is_ge, ALU.mult))
                step(V.tensor_scalar(mtmp[:, 1, :], mtmp[:, 1, :], -1.0, None, ALU.add))
                step(V.tensor_tensor(mrow[:, dst, :], mtmp[:, 0, :], mtmp[:, 1, :], ALU.mult))
            assert count[0] == SETUP_ROWS
            dve.wait_ge(setup_a, 2)
            step(V.tensor_tensor(neg_lam[:], lams[:, 1, :], lams[:, 0, :], ALU.subtract))
            step(V.tensor_scalar(neg_lam[:], neg_lam[:], -LAMBDA_INIT, None, ALU.add))
            assert count[0] == SETUP_DONE

            def take_max(b, h, n, rows):
                w, h8, bank = h // HU, h % HU, n % 2
                wait(dve, max_ps, b, n + 1)
                if n in (0, NBANKS // 2):
                    wait(dve, nm_step, b.plus(-1), 4 * (w + 1))
                if rows == 1:
                    m = V.reduce_max(mx[:, w, 1, :, h8:h8 + 1].rearrange("p t o -> p (t o)"),
                                     p_max[:, bank, :].rearrange("p (t k) -> p t k", t=2), AX.X)
                else:
                    m = V.reduce_max(mx[:, w, 0, :, h8 - 1:h8 + 1],
                                     p_max[:, bank, :].rearrange("p (t h k) -> p t h k", t=2, h=2), AX.X)
                m.then_inc(max_done.sem, 1)

            def minus_max(b, w, k):
                src = mx[:, w].rearrange("p a t h -> p (a t) h")
                if k == 0:
                    wait(dve, max_done, b, NBANKS // 2 * (w + 1))
                    wait(dve, nm_ps, b.plus(-1), w + 1)
                    ins = V.tensor_scalar(nm[:, w, :, 0, :], src, -1.0, None, ALU.mult)
                else:
                    wait(dve, nm_step, b, 4 * w + k)
                if k == 1:
                    ins = V.scalar_tensor_tensor(mrest[:], src, -1.0, nm[:, w, :, 0, :], ALU.mult, ALU.subtract)
                if k == 2:
                    ins = V.tensor_copy(nm[:, w, :, 1, :], mrest[:])
                if k == 3:
                    ins = V.tensor_tensor(nm[:, w, :, 2, :], mrest[:], nm[:, w, :, 1, :], ALU.subtract)
                ins.then_inc(nm_step.sem, 1)

            def rest_part(b, j):
                wait(dve, h_ready, b, j + 1)
                wait(dve, l_ready, b.plus(-1), j + 1)
                V.tensor_tensor(rest[:, j, :], p_mix[:, 0, :], part_h[:, j, :], ALU.subtract).then_inc(r_ready.sem, 1)

            def normalise(b, w, tile, bank, k):
                n = 2 * w + tile
                src = p_mix[:, bank, :].rearrange("p (h t d) -> p h t d", t=2, d=VW)
                r3 = rec[:].rearrange("p (h t) -> p h t", t=2)
                if k == 0:
                    wait(dve, ot_ps, b, n + 1)
                    wait(dve, on2_ready, b, n) if n else wait(dve, on2_ready, b.plus(-1))
                    V.reciprocal(r3, src[:, :, :, 2 * DH]).then_inc(rec_step.sem, 1)
                if k == 1:
                    wait(dve, rec_step, b, 2 * n + 1)
                    V.tensor_tensor(r3[:, :, 1], r3[:, :, 1], neg_lam[:, w * HU:(w + 1) * HU], ALU.mult).then_inc(rec_step.sem, 1)
                if k == 2:
                    wait(dve, rec_step, b, 2 * n + 2)
                    wait(dve, o_ready, b.plus(-1))
                    V.tensor_tensor(on2[:, tile, w * HU:(w + 1) * HU].rearrange("p h t d -> p (h t) d"),
                                    p_mix[:, bank, :].rearrange("p (j d) -> p j d", d=VW)[:, :, 0:2 * DH],
                                    rec[:].unsqueeze(2).to_broadcast([P, 2 * HU, 2 * DH]), ALU.mult).then_inc(on2_ready.sem, 1)

            def statistics(b, which, event):
                for tile in range(NT):
                    V.bn_stats(stats[:, which, tile, :], xres[:, bass.ds(b.n * SEQ + tile * DIM, DIM)]).then_inc(event.sem, 1)

            def mean_and_variance(b, which, event, tile):
                wait(dve, event, b, tile + 1)
                settle(dve)
                V.bn_aggr(mvs[:, which, tile, :], stats[:, which, tile, :]).then_inc(event.sem, 1)

            def inverse_roots(i, steps):
                bL, bC, bW = (i.plus(d) for d in (3, -1, -2))
                if not (active(bL) or active(bC) or active(bW)):
                    return
                done = NEWTON * (i.n + LEAD - 1)
                for k in steps:
                    if not i.static or done + k > 0:
                        dve.wait_ge(newton, done + k)
                    if k == 0:
                        if active(bC):
                            wait(dve, rms_sum, bC)
                        if active(bL):
                            wait(dve, stats1, bL)
                        if active(bW):
                            wait(dve, stats2, bW)
                        V.tensor_scalar(var[:, 0:NT * NH], rms_ss[:], 1.0 / (2 * DH), EPS, ALU.mult, ALU.add)
                        ins = V.tensor_scalar(var[:, NT * NH:NV], mvs[:].rearrange("p w t j -> p (w t) j")[:, :, 1], EPS, None, ALU.add)
                    elif k == 1:
                        ins = V.tensor_scalar(nt1[:].bitcast(I32), var[:].bitcast(I32), 1, None, ALU.logical_shift_right)
                    elif k == 2:
                        if active(bC.plus(-1)):
                            wait(dve, on_ready, bC.plus(-1))
                        if active(bL.plus(-1)):
                            wait(dve, xn_ready, bL.plus(-1))
                        if active(bW.plus(-1)):
                            wait(dve, xn2_ready, bW.plus(-1))
                        ins = V.tensor_scalar(rstd[:].bitcast(I32), nt1[:].bitcast(I32), -1.0, float(0x5F3759DF), ALU.mult, ALU.add)
                    elif k == 12:
                        ins = V.scalar_tensor_tensor(neg_mr[:], mvs[:].rearrange("p w t j -> p (w t) j")[:, :, 0], -1.0,
                                                     rstd[:, NT * NH:NV], ALU.mult, ALU.mult)
                    elif k % 3 == 0:
                        ins = V.tensor_tensor(nt1[:], rstd[:], rstd[:], ALU.mult)
                    elif k % 3 == 1:
                        ins = V.scalar_tensor_tensor(nt2[:], nt1[:], -0.5, var[:], ALU.mult, ALU.mult)
                    else:
                        ins = V.scalar_tensor_tensor(rstd[:], nt2[:], 1.5, rstd[:], ALU.add, ALU.mult)
                    ins.then_inc(newton, 1)

            def body(i):
                bL, bA, bV, b1, b2, bC, bW, bR = (i.plus(d) for d in (3, 2, 1, 1, 0, -1, -2, -3))
                if i.static and i.c >= NB:
                    if i.c == NB:
                        dve.wait_ge(ffn_w_loaded, 48)
                        dve.wait_ge(exp_ps.sem, NBANKS * NB)
                    for c in range(2):
                        split_weights(dve, 2 * (i.c - NB) + c)
                for s in range(NH):
                    n = s + s // 2
                    if active(b1):
                        take_max(b1, s, n, 1)
                    if s < 2 and active(b2):
                        minus_max(b2, 1, s)
                    if s == 0 and active(bW):
                        dve.wait_ge(newton, NEWTON * (i.n + LEAD - 1) - 1)
                        wait(dve, ont_ps, bW.plus(-1))
                        V.tensor_tensor(on_tok[:].rearrange("p t (h d) -> p (t h) d", d=2 * DH), o[:],
                                        rstd[:, 0:NT * NH].unsqueeze(2).to_broadcast([P, NT * NH, 2 * DH]),
                                        ALU.mult).then_inc(on_ready.sem, 1)
                    if s == 2 and active(b2):
                        minus_max(b2, 1, 3)
                    if s == 2 and active(bA):
                        rest_part(bA, 0)
                    if s == 3 and active(bW):
                        wait(dve, wo_ps, bW)
                        wait_half(dve, mods_loaded[bW.par], bW)
                        wait(dve, x1_ready, bW.plus(-1))
                        V.tensor_tensor(xtmp[:], p_mix[:, 1, 0:SEQ].rearrange("p (t c) -> p t c", t=NT),
                                        mods[:, bW.par, 0:1, :].to_broadcast([P, NT, DIM]), ALU.mult).then_inc(attn_scaled.sem, 1)
                    if s == 4 and active(bA):
                        rest_part(bA, 1)
                    if s == 4 and active(bL):
                        wait_half(dve, x_loaded[bL.par], bL)
                        settle(dve)
                        statistics(bL, 0, stats1)
                    if s == 5:
                        for k in range(3):
                            if active(bC):
                                normalise(bC, 1, 0, 1, k)
                            if k < NT and active(bL):
                                mean_and_variance(bL, 0, stats1, k)
                    if s == 6 and active(bC):
                        for k in range(3):
                            normalise(bC, 1, 1, 0, k)
                    if s == 6 and active(bW):
                        wait(dve, x1_ready, bW)
                        settle(dve)
                        statistics(bW, 1, stats2)
                    if s == 7 and active(bW):
                        for tile in range(NT):
                            mean_and_variance(bW, 1, stats2, tile)
                    if s == 8:
                        if active(bR):
                            wait(dve, route, bR.plus(-1))
                            wait(dve, lg_ps, bR)
                            V.tensor_tensor(lg[:], p_mix[:, 1, 0:NT * NE].rearrange("p (t e) -> p t e", t=NT),
                                            rb[:].unsqueeze(1).to_broadcast([P, NT, NE]), ALU.add).then_inc(route.sem, 1)
                        if active(b1):
                            minus_max(b1, 0, 0)
                        if active(bR):
                            wait(dve, route, bR, 1)
                            settle(dve)
                            for tile in range(NT):
                                V.max(top8[:, tile, :], lg[:, tile, :]).then_inc(route.sem, 1)
                        if active(b1):
                            minus_max(b1, 0, 1)
                        if active(bR):
                            wait(dve, route, bR, 3)
                            settle(dve)
                            for tile in range(NT):
                                V.max_index(top8i[:, tile, :], top8[:, tile, :], lg[:, tile, :]).then_inc(route.sem, 1)
                            V.tensor_tensor(gdiff[:], top8[:, :, 1], top8[:, :, 0], ALU.subtract).then_inc(route.sem, 1)
                        if active(b1):
                            minus_max(b1, 0, 2)
                        if active(bR):
                            wait(dve, route, bR, 5)
                            V.tensor_copy(topf[:].rearrange("p j t -> p t j"), top8i[:, :, 0:2]).then_inc(route.sem, 1)
                        if active(b1):
                            minus_max(b1, 0, 3)
                        if active(bR):
                            wait(dve, route, bR, 7)
                            V.tensor_tensor(chosen[:], iota8[:].unsqueeze(1).to_broadcast([P, 2 * NT, NE]),
                                            topf[:].rearrange("p j t -> p (j t)").unsqueeze(2).to_broadcast([P, 2 * NT, NE]),
                                            ALU.is_equal).then_inc(route.sem, 1)
                    if s == 9 and active(bR):
                        wait(dve, route, bR, 8)
                        V.tensor_tensor(both[:], chosen[:, 0:NT, :], chosen[:, NT:2 * NT, :], ALU.add).then_inc(route.sem, 1)
                    if s == 10 and active(bC):
                        wait(dve, osq_ready, bC)
                        V.reduce_sum(rms_ss[:], osq[:], AX.X).then_inc(rms_sum.sem, 1)
                    if s == 11:
                        inverse_roots(i, [0])
                        if active(bR):
                            wait(dve, rank_ps, bR)
                            V.tensor_tensor(pos[:], p_mix[:, 1, 0:NT * NE].rearrange("p (t e) -> p t e", t=NT),
                                            carry[:].unsqueeze(1).to_broadcast([P, NT, NE]), ALU.add).then_inc(route.sem, 1)
                            wait(dve, gexp_ready, bR)
                            V.tensor_scalar(gden[:], gexp[:], 1.0, None, ALU.add).then_inc(route.sem, 1)
                        inverse_roots(i, [1])
                        if active(bR):
                            wait(dve, route, bR, 10)
                            V.tensor_tensor(carry[:], carry[:], p_mix[:, 1, 2 * NE:3 * NE], ALU.add).then_inc(route.sem, 1)
                            for j in range(2):
                                ins = V.tensor_tensor(posm[:, j * NT:(j + 1) * NT, :], chosen[:, j * NT:(j + 1) * NT, :], pos[:], ALU.mult)
                            ins.then_inc(route.sem, 1)
                    if s == 12:
                        inverse_roots(i, [2])
                        hrow = h2[:, bR.par].rearrange("p j t r -> p (j t) r")
                        if active(bR):
                            wait(dve, route, bR, 11)
                            V.reciprocal(hrow[:, 0:NT, DIM + 1], gden[:]).then_inc(route.sem, 1)
                        inverse_roots(i, [3])
                        if active(bR):
                            wait(dve, route, bR, 13)
                            V.reduce_sum(posf[:], posm[:], AX.X).then_inc(route.sem, 1)
                        inverse_roots(i, [4])
                        if active(bR):
                            wait(dve, route, bR, 14)
                            V.tensor_tensor(hrow[:, NT:2 * NT, DIM + 1], hrow[:, 0:NT, DIM + 1], gexp[:], ALU.mult)
                            V.tensor_copy(hrow[:, :, DIM].bitcast(I32), pairno[:])
                            wait(dve, route, bR, 15)
                            V.tensor_copy(idx[:, bR.par, :], posf[:]).then_inc(route.sem, 1)
                        inverse_roots(i, [5])
                    if s == 13:
                        inverse_roots(i, [6])
                        if active(b2):
                            normalise(b2, 0, 0, 0, 0)
                        inverse_roots(i, [7])
                        if active(b2):
                            normalise(b2, 0, 0, 0, 1)
                        inverse_roots(i, [8])
                        if active(b2):
                            normalise(b2, 0, 0, 0, 2)
                    if s == 14:
                        inverse_roots(i, [9, 10, 11, 12])
                    if s == 15:
                        for k in range(3):
                            if active(b2):
                                normalise(b2, 0, 1, 1, k)
                            if k == 0 and active(bR):
                                wait(dve, route, bR, ROUTE_ROWS)
                                V.tensor_scalar(pairno[:], pairno[:], float(SEQ), None, ALU.add).then_inc(route.sem, 1)
                    if active(b1) and s % 2:
                        take_max(b1, s, n + 1, 0)
                    if s == 1 and active(b2):
                        minus_max(b2, 1, 2)

            iterations(dve, body)
            ffn_vector(dve)

        @block.gpsimd
        def _(pool):
            G = nc.gpsimd
            zero = G.to_reg(0.0)
            G.memset(v[:], 0.0).then_inc(setup_g, 1)
            pool.wait_ge(setup_g, 1)
            G.memset(v[:, :, :, :, 2 * DH:2 * DH + 1], 1.0).then_inc(setup_g, 1)
            G.memset(kt[0:QK_ROWS].rearrange("p a t h k -> p (a t h k)").bitcast(F32), 0.0)

            def mask_bank(b, n):
                g, k = n // 3, n % 3
                wait(pool, exp_done, b, n + 1)
                settle(pool)
                blocks = (probs[:, g % 2, k, :].rearrange("p (t k) -> p t k", t=2)[:, :, 0:P] if k < 2
                          else probs[:, g % 2, k, :].rearrange("p (t k) -> p t k", t=4))
                G.affine_select(out=blocks, in_=blocks, compare_op=ALU.is_ge, fill=zero, base=0,
                                pattern=[[0, 2 if k < 2 else 4], [1, P]], channel_multiplier=-1).then_inc(masked.sem, 1)

            def low_part(b, j):
                wait(pool, m_ready, b, j + 1)
                wait(pool, parts_saved, b.plus(-1))
                G.tensor_tensor(part_l[:, j, :], rest[:, j, :], part_m[:, j, :], ALU.subtract).then_inc(l_ready.sem, 1)

            def body(i):
                bA, b2, bC, bW, bR = (i.plus(d) for d in (2, 0, -1, -2, -3))
                for s in range(NH):
                    if active(b2):
                        mask_bank(b2, s + s // 2)
                        if s % 2:
                            mask_bank(b2, s + s // 2 + 1)
                    if s == 4 and active(bW):
                        wait(pool, attn_scaled, bW)
                        xb = xres[:, bass.ds(bW.n * SEQ, SEQ)]
                        G.tensor_tensor(xb, xb, xtmp[:].rearrange("p t c -> p (t c)"), ALU.add).then_inc(x1_ready.sem, 1)
                    if s in (4, 6) and active(bA):
                        low_part(bA, (s - 4) // 2)
                    if s == 0 and active(bR):
                        wait(pool, xn2_ready, bR)
                        wait_half(pool, mods_loaded[bR.par], bR)
                        hb = h2[:, bR.par, 0, :, 0:DIM]
                        G.tensor_tensor(hb, hb, mods[:, bR.par, 1:2, :].to_broadcast([P, NT, DIM]), ALU.mult).then_inc(h2_step.sem, 1)
                    if s == 2 and active(bR):
                        wait(pool, h2_step, bR, 1)
                        hb = h2[:, bR.par, 0, :, 0:DIM]
                        G.tensor_tensor(hb, hb, mods[:, bR.par, 2:3, :].to_broadcast([P, NT, DIM]), ALU.add).then_inc(h2_step.sem, 1)
                    if s == 7 and active(bC):
                        wait(pool, on2_ready, bC)
                        wait(pool, on_ready, bC.plus(-1))
                        a = on2[:].rearrange("p a h t d -> p (a h) t d")
                        G.tensor_tensor(o[:], a[:, :, 0, :], a[:, :, 1, :], ALU.add).then_inc(o_ready.sem, 1)
                    if s == 8 and active(bC):
                        wait(pool, o_ready, bC)
                        wait(pool, rms_sum, bC.plus(-1))
                        G.tensor_tensor(osq[:], o[:], o[:], ALU.mult).then_inc(osq_ready.sem, 1)
                    if s in (12, 13, 14, 15) and active(bR):
                        k = s - 12
                        if k == 0:
                            wait(pool, route, bR, ROUTE_ROWS)
                            wait(pool, h2_copied, bR)
                            settle(pool)
                        G.indirect_dma_start(rows_sorted, bass.IndirectOffsetOnAxis(idx[:, bR.par, k:k + 1].bitcast(U32), 0),
                                             h2[:, bR.par, k // NT, k % NT, :], None).then_inc(scattered[bR.par].sem, 16)

            iterations(pool, body)
            ffn_pool(pool)


def kernel(L0_attn_X, L0_attn_W_q, L0_attn_W_k, L0_attn_W_v, L0_attn_W_o, L0_attn_lambda_q1, L0_attn_lambda_k1,
           L0_attn_lambda_q2, L0_attn_lambda_k2, L0_attn_rms_scale, L0_ffn_router_w, L0_ffn_router_b, L0_ffn_gate_w,
           L0_ffn_up_w, L0_ffn_down_w, L0_c, L0_wmod):
    import concourse.bacc as bacc
    from concourse.bass_utils import run_bass_kernel_spmd

    def lay(a):
        return np.ascontiguousarray(np.asarray(a))

    def halves(w):
        return lay(w).reshape(NH, 2, DH, DIM).transpose(3, 1, 2, 0).reshape(DIM, 2, DH * NH)

    def up_layout(w):
        return lay(w).transpose(2, 0, 1).reshape(DIM, NE * FF)

    p = np.arange(P)
    fill_row = np.zeros((P, RW), np.float32)
    fill_row[:, DIM] = np.full(P, SKIPPED, np.int32).view(np.float32)
    max_ones = np.zeros((2, 3, 4, 2, HU * SEQ // 2), np.int32)
    for t in range(2):
        max_ones[t, :, :, t] = 0x3F803F80
    arrays = {
        "x": lay(L0_attn_X),
        "w_qk": lay(np.concatenate([halves(L0_attn_W_q), halves(L0_attn_W_k)], axis=1)),
        "w_v": lay(lay(L0_attn_W_v).T),
        "w_o": lay(lay(L0_attn_W_o).T.reshape(2, P, DIM).transpose(1, 0, 2)),
        "lambdas": lay(np.stack([np.broadcast_to(lay(a).reshape(-1), (P, NH * DH)) for a in
                                 (L0_attn_lambda_q1, L0_attn_lambda_k1, L0_attn_lambda_q2, L0_attn_lambda_k2)])),
        "rms_col": lay(np.tile(lay(L0_attn_rms_scale), P // (2 * DH)).reshape(P, 1)),
        "router_w": lay(lay(L0_ffn_router_w).T),
        "router_b": lay(np.broadcast_to(lay(L0_ffn_router_b), (P, NE))),
        "gate_w": lay(up_layout(L0_ffn_gate_w)),
        "up_w": lay(up_layout(L0_ffn_up_w)),
        "down_w": lay(lay(L0_ffn_down_w).reshape(NE, DIM, FCH, P).transpose(3, 0, 2, 1).reshape(P, NE * FF)),
        "c_t": lay(lay(L0_c).T),
        "w_mod": lay(L0_wmod),
        "max_ones": max_ones.reshape(MAX_ROWS, 4, 2, HU * SEQ // 2),
        "ident": np.eye(P, dtype=np.float32),
        "mask_q": np.where(p[None, :] <= p[:, None], 0.0, NEG).astype(np.float32),
        "before": (p[:, None] < p[None, :]).astype(np.float32),
        "iota": lay(np.broadcast_to(np.arange(NE, dtype=np.float32), (P, NE))),
        "ramp": lay(np.broadcast_to(np.arange(NE, dtype=np.float32) * REGION, (P, NE))),
        "pair_no": (p[:, None] + np.array([[j * NB * SEQ + t * P for j in range(2) for t in range(NT)]])).astype(np.float32),
        "tile_no": lay(np.broadcast_to(np.arange(FFN_TILES, dtype=np.float32), (P, FFN_TILES))),
        "filler": fill_row,
    }
    nc = bacc.Bacc("TRN2", target_bir_lowering=False, num_devices=1)
    args = {n: nc.dram_tensor(f"in_{n}", a.shape, mybir.dt.from_np(a.dtype), kind="ExternalInput").ap()
            for n, a in arrays.items()}
    out = nc.dram_tensor("out_dram", (NB, SEQ, DIM), F32, kind="ExternalOutput").ap()
    adaln_block(nc, out=out, **args)
    r = run_bass_kernel_spmd(nc, [{f"in_{n}": a for n, a in arrays.items()}], core_ids=[0])
    return r.results[0]["out_dram"]
```
